# Optimizing a Trainium2 kernel written in Bass

```python
import numpy as np
import jax
import jax.numpy as jnp

def _softmax(x, axis=-1):
    return jax.nn.softmax(x, axis=axis)

def _gelu(x):
    return jax.nn.gelu(x, approximate=True)

def _silu(x):
    return jax.nn.silu(x)

def _sigmoid(x):
    return jax.nn.sigmoid(x)

def _layernorm(x, axis=-1, eps=1e-05):
    m = jnp.mean(x, axis=axis, keepdims=True)
    v = jnp.var(x, axis=axis, keepdims=True)
    return (x - m) / jnp.sqrt(v + eps)

def _scatter_add(tgt, idx, src, axis=0):
    return tgt.at[idx].add(src)

def _segment_sum(src, seg, n):
    return jax.ops.segment_sum(src, seg, n)
kernel_name = 'mk_conv_attn_hybrid_d2_conv_nhwc1024_r4_ac42e3'

def setup_inputs(seed: int=0):
    np.random.seed(seed)
    _w = jnp.asarray

    def _rec_inputs():
        import jax
        import jax.numpy as jnp
        _gk = jax.random.key(seed)
        x = -7.109e-05 + 0.9999 * jax.random.normal(jax.random.fold_in(_gk, 1), (16, 16, 16, 256), jnp.float32)
        return x
    x = _rec_inputs()

    def _L0_conv_setup():
        import jax, jax.numpy as jnp
        import numpy as np
        import math
        B, T, IN_CH, OUT_CH, L = (16, 16, 16, 16, 256)
        MODES = 16
        HEADS = 4
        MIDCH = 32
        C_CONST = 1.0

        def timestep_embedding(t, dim):
            half = dim // 2
            freqs = jnp.exp(-math.log(10000.0) * jnp.arange(half, dtype=jnp.float32) / half)
            args = t[:, None] * freqs[None, :]
            return jnp.concatenate([jnp.sin(args), jnp.cos(args)], axis=-1)
        key = jax.random.key(seed)
        k1, k2, k3, k4 = jax.random.split(key, 4)
        scale_w = 1.0 / (IN_CH * OUT_CH)
        scale_e = 1.0 / (MIDCH * MODES)
        x = jax.random.normal(k1, (B, T, IN_CH, L), dtype=jnp.float32)
        t = jax.random.uniform(k2, (T,), dtype=jnp.float32) * 1000.0
        weights1 = scale_w * jax.random.uniform(k3, (IN_CH, OUT_CH, MODES, 2), dtype=jnp.float32)
        ke_weights = scale_e * jax.random.uniform(k4, (HEADS, MIDCH // HEADS, 2 * MODES), dtype=jnp.float32)
        ke_bias = jnp.zeros((1, 1, 2 * MODES), dtype=jnp.float32)
        return {'x': x, 't': t, 'weights1': weights1, 'ke_weights': ke_weights, 'ke_bias': ke_bias}
    _L0_conv_all = _L0_conv_setup()
    _L0_conv_in = {k: v for k, v in _L0_conv_all.items() if k in ('t', 'weights1', 'ke_weights', 'ke_bias')}
    del _L0_conv_all

    def _L1_attn_setup():
        import jax, jax.numpy as jnp
        import numpy as np
        D_MODEL = 256
        key = jax.random.key(seed)
        kx, kq, kk, kv, ko = jax.random.split(key, 5)
        s = 1.0 / np.sqrt(D_MODEL)
        return {'x': jax.random.normal(kx, (4, 1024, D_MODEL), dtype=jnp.float32), 'W_q': jax.random.normal(kq, (D_MODEL, D_MODEL), dtype=jnp.float32) * s, 'W_k': jax.random.normal(kk, (D_MODEL, D_MODEL), dtype=jnp.float32) * s, 'W_v': jax.random.normal(kv, (D_MODEL, D_MODEL), dtype=jnp.float32) * s, 'W_o': jax.random.normal(ko, (D_MODEL, D_MODEL), dtype=jnp.float32) * s}
    _L1_attn_all = _L1_attn_setup()
    _L1_attn_in = {k: v for k, v in _L1_attn_all.items() if k in ('W_q', 'W_k', 'W_v', 'W_o')}
    del _L1_attn_all

    def _L1_ffn_setup():
        import jax, jax.numpy as jnp
        import numpy as np
        B, S, D = (4, 512, 256)
        E, K = (8, 2)
        DFF = 4 * D
        key = jax.random.key(seed)
        k1, k2, k3, k4 = jax.random.split(key, 4)
        x = jax.random.normal(k1, (B, S, D), dtype=jnp.float32)
        router_w = jax.random.normal(k2, (D, E), dtype=jnp.float32) * (1.0 / np.sqrt(D))
        w_fc = jax.random.normal(k3, (E, D, DFF), dtype=jnp.float32) * (1.0 / np.sqrt(D))
        w_proj = jax.random.normal(k4, (E, DFF, D), dtype=jnp.float32) * (1.0 / np.sqrt(DFF))
        return {'x': x, 'router_w': router_w, 'w_fc': w_fc, 'w_proj': w_proj}
    _L1_ffn_all = _L1_ffn_setup()
    _L1_ffn_in = {k: v for k, v in _L1_ffn_all.items() if k in ('router_w', 'w_fc', 'w_proj')}
    del _L1_ffn_all
    return {'x': x, 'L0_conv_t': _L0_conv_in['t'], 'L0_conv_weights1': _L0_conv_in['weights1'], 'L0_conv_ke_weights': _L0_conv_in['ke_weights'], 'L0_conv_ke_bias': _L0_conv_in['ke_bias'], 'L1_attn_W_q': _L1_attn_in['W_q'], 'L1_attn_W_k': _L1_attn_in['W_k'], 'L1_attn_W_v': _L1_attn_in['W_v'], 'L1_attn_W_o': _L1_attn_in['W_o'], 'L1_ffn_router_w': _L1_ffn_in['router_w'], 'L1_ffn_w_fc': _L1_ffn_in['w_fc'], 'L1_ffn_w_proj': _L1_ffn_in['w_proj']}

def reference(x, L0_conv_t, L0_conv_weights1, L0_conv_ke_weights, L0_conv_ke_bias, L1_attn_W_q, L1_attn_W_k, L1_attn_W_v, L1_attn_W_o, L1_ffn_router_w, L1_ffn_w_fc, L1_ffn_w_proj):
    import jax
    import jax.numpy as jnp

    def _L0_conv_ref(x, t, weights1, ke_weights, ke_bias):
        import jax, jax.numpy as jnp
        import numpy as np
        import math
        B, T, IN_CH, OUT_CH, L = (16, 16, 16, 16, 256)
        MODES = 16
        HEADS = 4
        MIDCH = 32
        C_CONST = 1.0

        def timestep_embedding(t, dim):
            half = dim // 2
            freqs = jnp.exp(-math.log(10000.0) * jnp.arange(half, dtype=jnp.float32) / half)
            args = t[:, None] * freqs[None, :]
            return jnp.concatenate([jnp.sin(args), jnp.cos(args)], axis=-1)
        emb = timestep_embedding(t, MIDCH)
        thc = emb.reshape(T, HEADS, MIDCH // HEADS)
        thm = jnp.einsum('thc,hcm->thm', thc, ke_weights)
        thm = jnp.tile(thm, (1, IN_CH // HEADS, 1)) + ke_bias
        wt = thm.reshape(T, IN_CH, MODES, 2)
        w_temb = wt[..., 0] + 1j * wt[..., 1]
        w = weights1[..., 0] + 1j * weights1[..., 1]
        x_ft = jnp.fft.rfft(x, axis=-1)[..., :MODES]
        out = x_ft * w_temb[None]
        out = jnp.einsum('btix,iox->btox', out, w)
        norm = jnp.einsum('tix,iox->tox', jnp.abs(w_temb), jnp.abs(w)) + 1e-12
        norm = jax.nn.relu(norm / C_CONST - 1.0) + 1.0
        out = out / norm[None]
        nf = L // 2 + 1
        out_ft = jnp.zeros((B, T, OUT_CH, nf), dtype=out.dtype).at[..., :MODES].set(out)
        return jnp.fft.irfft(out_ft, n=L, axis=-1)

    def _L1_attn_ref(x, W_q, W_k, W_v, W_o):
        import jax, jax.numpy as jnp
        import numpy as np
        D_MODEL = 256
        B, T, D = x.shape
        q = jnp.einsum('btd,ed->bte', x, W_q)
        k = jnp.einsum('btd,ed->bte', x, W_k)
        v = jnp.einsum('btd,ed->bte', x, W_v)
        scale = 1.0 / jnp.sqrt(jnp.asarray(D, x.dtype))
        scores = jnp.einsum('bqd,bkd->bqk', q, k) * scale
        causal = jnp.tril(jnp.ones((T, T), dtype=bool))
        scores = jnp.where(causal, scores, -jnp.inf)
        att = jax.nn.softmax(scores, axis=-1)
        y = jnp.einsum('bqk,bkd->bqd', att, v)
        out = jnp.einsum('btd,ed->bte', y, W_o)
        return out

    def _L1_ffn_ref(x, router_w, w_fc, w_proj):
        import jax, jax.numpy as jnp
        import numpy as np
        B, S, D = (4, 512, 256)
        E, K = (8, 2)
        DFF = 4 * D
        b, s, d = x.shape
        flat_x = x.reshape(b * s, d)
        router_logits = flat_x @ router_w
        router_probs = jax.nn.softmax(router_logits, axis=-1)
        topk_w, topk_idx = jax.lax.top_k(router_probs, K)
        topk_w = topk_w / jnp.sum(topk_w, axis=-1, keepdims=True)
        combine = jnp.sum(jax.nn.one_hot(topk_idx, E, dtype=flat_x.dtype) * topk_w[..., None], axis=1)
        out = jnp.zeros_like(flat_x)
        for e in range(E):
            h = jax.nn.gelu(flat_x @ w_fc[e], approximate=False)
            out = out + combine[:, e:e + 1] * (h @ w_proj[e])
        return out.reshape(b, s, d)

    def _gn(v, G=32, eps=1e-05):
        B_, H_, W_, C_ = v.shape
        g = v.reshape(B_, H_, W_, G, C_ // G)
        m = jnp.mean(g, axis=(1, 2, 4), keepdims=True)
        s = jnp.var(g, axis=(1, 2, 4), keepdims=True)
        return ((g - m) / jnp.sqrt(s + eps)).reshape(v.shape)

    def _ln_c(v, eps=1e-06):
        m = jnp.mean(v, axis=-1, keepdims=True)
        s = jnp.var(v, axis=-1, keepdims=True)
        return (v - m) / jnp.sqrt(s + eps)

    def _ln_t(v, eps=1e-05):
        m = jnp.mean(v, axis=-1, keepdims=True)
        s = jnp.var(v, axis=-1, keepdims=True)
        return (v - m) / jnp.sqrt(s + eps)

    def _to_tokens(v):
        B_, H_, W_, C_ = v.shape
        return v.reshape(B_, H_ * W_, C_)

    def _from_tokens(t, like):
        return t.reshape(like.shape)
    x = x + _L0_conv_ref(_gn(x), L0_conv_t, L0_conv_weights1, L0_conv_ke_weights, L0_conv_ke_bias)
    t = _to_tokens(x)
    t = t + _L1_attn_ref(_ln_t(t), L1_attn_W_q, L1_attn_W_k, L1_attn_W_v, L1_attn_W_o)
    t = t + _L1_ffn_ref(_ln_t(t), L1_ffn_router_w, L1_ffn_w_fc, L1_ffn_w_proj)
    x = _from_tokens(t, x)
    return x

_drawn_inputs = setup_inputs


def setup_inputs(seed=0):
    import zlib

    import numpy as np

    out = dict(_drawn_inputs(seed))
    spreads = {'L0_conv_ke_bias': (0.0, 0.8)}
    factors = {'L0_conv_t': 43.902, 'L0_conv_weights1': 8.0, 'L0_conv_ke_weights': 200.0}
    for name, (base, spread) in spreads.items():
        noise = np.random.default_rng([zlib.crc32(name.encode()), seed]).standard_normal(out[name].shape)
        drawn = base * np.exp(spread * noise) if base else spread * noise
        out[name] = jnp.asarray(drawn.astype(out[name].dtype))
    for name, factor in factors.items():
        out[name] = (out[name] * factor).astype(out[name].dtype)
    return out
```

```python
from contextlib import ExitStack

import numpy as np
import concourse.bass as bass
from concourse import mybir

F32 = mybir.dt.float32
ALU = mybir.AluOpType
ACT = mybir.ActivationFunctionType
AX_X = mybir.AxisListType.X

P = 128
B, HT, WI, D = 16, 16, 16, 256
TOK = B * HT * WI
SEQ = HT * WI
NT = TOK // P
DH = D // P
MODES = 16
MC = 2 * MODES
NG = WI * MC // P
HEADS, MIDCH = 4, 32
GN_EPS, LN_EPS = 1e-5, 1e-5
E, DFF = 8, 1024
FC = DFF // P
TT = 512
NTT = TOK // TT

MASKED = -1e30
MAGIC = 1.5 * 2.0 ** 23
TWO_PI = 2.0 * np.pi
PI_LOW = 3.1415925


def two_pi_parts():
    parts, rest = [], TWO_PI
    for _ in range(3):
        step = 2.0 ** (np.floor(np.log2(rest)) - 8)
        parts.append(float(np.floor(rest / step) * step))
        rest -= parts[-1]
    return parts + [float(np.float32(rest))]


def constants():
    l = np.arange(D)
    x = np.arange(MODES)
    angle = 2 * np.pi * np.outer(l, x) / D
    dft = np.stack([np.cos(angle), -np.sin(angle)], axis=-1).reshape(D, MC)
    weight = np.where(x == 0, 1.0, 2.0)[:, None] / D
    idft = np.stack([np.cos(angle.T) * weight, -np.sin(angle.T) * weight], axis=1).reshape(MC, D)
    same_mode = np.repeat(np.repeat(np.eye(MODES), 2, 0), 2, 1)
    c, c2 = np.arange(MC)[:, None] % 2, np.arange(MC)[None, :] % 2
    sign_r = np.where((c == 1) & (c2 == 0), -1.0, 1.0)
    sign_i = np.where((c == 0) & (c2 == 1), 1.0, -1.0)
    masks = np.stack([same_mode * sign_r, same_mode * sign_i, same_mode * (c == 0)], axis=1)
    masks = np.tile(masks, (4, 1, 1))
    q, k = np.arange(P)[:, None], np.arange(P)[None, :]
    causal = np.concatenate([np.zeros((P, P)), np.where(k <= q, 0.0, MASKED)], axis=1)
    half = MIDCH // 2
    steps = -np.float32(np.log(10000.0)) * np.arange(half, dtype=np.float32) / np.float32(half)
    freqs = np.exp(steps.astype(np.float64)).astype(np.float32)
    angles = np.stack([np.tile(freqs, 2), np.repeat([1.0, 0.0], half), np.repeat([0.0, 1.0], half)], axis=1)
    f = np.float32
    return {
        "c_dft": dft.astype(f), "c_idft": idft.astype(f), "c_masks": masks.astype(f),
        "c_causal": causal.astype(f), "c_ident": np.eye(P, dtype=f),
        "c_group": np.kron(np.eye(P // 8), np.full((8, 8), 1 / 8)).astype(f),
        "c_angles": angles.astype(f),
    }


def hybrid_block(nc, x_tok_d, x_ch_d, t_d, mixr_w_d, mixi_w_d, temb_rw_d, temb_iw_d, bias_d, wq_d, wk_d, wv_d, wo_t_d,
                 router_d, w_fc_d, w_proj_d, c_dft_d, c_idft_d, c_masks_d, c_causal_d, c_ident_d, c_group_d,
                 c_angles_d, out_d):
    with ExitStack() as ctx:
        def sb(name, shape, dt=F32):
            return ctx.enter_context(nc.sbuf_tensor(name, shape, dt))

        def ps(name):
            return ctx.enter_context(nc.psum_tensor(name, [P, 512], F32))

        def sem(name):
            return ctx.enter_context(nc.semaphore(name))

        x = sb("x", [P, NT, D])
        xc = sb("xc", [P, DH, TOK])
        ident = sb("ident", [P, P])
        causal = sb("causal", [P, SEQ])
        dft = sb("dft", [P, DH, MC])
        idft = sb("idft", [MC, D])
        masks = sb("masks", [P, 3, MC])
        group = sb("group", [P, P])
        angles = sb("angles", [MIDCH, 3])
        wq, wk, wv, wo_t = (sb(n, [P, DH, D]) for n in ("wq", "wk", "wv", "wo_t"))
        router = sb("router", [P, DH, E])
        mixr_w = sb("mixr_w", [P, NG, WI, 2])
        mixi_w = sb("mixi_w", [P, NG, WI, 2])
        mix_r = sb("mix_r", [P, NG, WI, MODES, 2])
        mix_i = sb("mix_i", [P, NG, WI, MODES, 2])
        mix_abs = sb("mix_abs", [P, NG, WI, MODES, 2])
        sq = sb("sq", [P, NG * WI, 2])
        wabs = sb("wabs", [P, NG * WI])
        temb_rw = sb("temb_rw", [MIDCH, P])
        temb_iw = sb("temb_iw", [MIDCH, P])
        bias = sb("bias", [P, 2])
        t_row = sb("t_row", [MIDCH, HT])
        ang = sb("ang", [MIDCH, 4, HT])
        emb = sb("emb", [MIDCH, HT])
        temb = sb("temb", [P, 2, HT])
        tsq = sb("tsq", [P, 2, HT])
        tabs = sb("tabs", [P, HT])
        inv = sb("inv", [P, NG * HT])
        gst = sb("gst", [P, 8, 6])
        gmv = sb("gmv", [P, 8, 2])
        ggm = sb("ggm", [P, 8, 2])
        gtmp = sb("gtmp", [P, 3, 8])
        zr = sb("zr", [P, NG, B, HT])
        zi = sb("zi", [P, NG, B, HT])
        spec = sb("spec", [MC, TOK])
        qk_w = sb("qk_w", [P, DH, D])
        vo_w = sb("vo_w", [P, DH, D])
        spec_b = sb("spec_b", [MC, SEQ])
        st1, st2 = sb("st1", [P, 2, 6]), sb("st2", [P, 2, 6])
        mv1, mv2 = sb("mv1", [P, 2, 2]), sb("mv2", [P, 2, 2])
        rs1, rs2 = sb("rs1", [P, 2]), sb("rs2", [P, 2])
        xn = sb("xn", [P, 2, D])
        xn2 = sb("xn2", [P, 2, D])
        xn_t = sb("xn_t", [P, DH, SEQ])
        xn2_t = sb("xn2_t", [P, DH, SEQ])
        g_t = sb("g_t", [P, DH, SEQ])
        v_b = sb("v_b", [P, 2, D])
        s_b = sb("s_b", [P, 3 * P])
        p_b = sb("p_b", [P, 3 * P])
        p_t = sb("p_t", [P, 3 * P])
        nmax = sb("nmax", [P, 2])
        rsum = sb("rsum", [P, 2])
        rinv = sb("rinv", [P, 2])
        logits = sb("logits", [P, NT, E])
        hot = sb("hot", [P, 4, NT, E])
        top = sb("top", [P, 4, NT])
        combine = sb("combine", [P, NT, E])
        fc = sb("fc", [P, DH, DFF])
        proj = sb("proj", [P, FC, D])
        h = sb("h", [P, FC, TT])

        psT1, psT2, psG, psV, psS, psP, psO, psI = banks = [ps(n) for n in (
            "psT1", "psT2", "psG", "psV", "psS", "psP", "psO", "psI")]
        ld_emb, ld_x, ld_qkvo, ld_gn, ld_conv, ld_attn = (
            sem(n) for n in ("ld_emb", "ld_x", "ld_qkvo", "ld_gn", "ld_conv", "ld_attn"))
        ld_xc = [sem(f"ld_xc{c}") for c in range(4)]
        emb_step, emb_ready, sin_ready, temb_mm, temb_step, temb_ready = (
            sem(n) for n in ("emb_step", "emb_ready", "sin_ready", "temb_mm", "temb_step", "temb_ready"))
        mix_built, wabs_step, wabs_ready, norm_mm, inv_step, inv_ready = (
            sem(n) for n in ("mix_built", "wabs_step", "wabs_ready", "norm_mm", "inv_step", "inv_ready"))
        qkvo_mm, qkvo_ready = sem("qkvo_mm"), sem("qkvo_ready")
        gn_step, gn_stats, gn_mm, gn_done = (sem(n) for n in ("gn_step", "gn_stats", "gn_mm", "gn_done"))
        dft_mm, z_ready, mix_mm, spec_ready = (sem(n) for n in ("dft_mm", "z_ready", "mix_mm", "spec_ready"))
        spec_copied, idft_mm, x1_ready, ln1_step, xn_ready = (
            sem(n) for n in ("spec_copied", "idft_mm", "x1_ready", "ln1_step", "xn_ready"))
        t1_mm, xnt_ready, g_mm, gt_ready, v_mm, v_ready, s_mm = (
            sem(n) for n in ("t1_mm", "xnt_ready", "g_mm", "gt_ready", "v_mm", "v_ready", "s_mm"))
        s_masked, nmax_ready, probs_ready, pt_mm, pt_ready, pv_mm, rinv_ready = (
            sem(n) for n in ("s_masked", "nmax_ready", "probs_ready", "pt_mm", "pt_ready", "pv_mm", "rinv_ready"))
        x2_ready, ln2_step, xn2_ready, t2_mm, xn2t_ready, r_mm, logits_ready, xn2t_kept = (
            sem(n) for n in ("x2_ready", "ln2_step", "xn2_ready", "t2_mm", "xn2t_ready", "r_mm", "logits_ready", "xn2t_kept"))
        csel_ready, top_exp = sem("csel_ready"), sem("top_exp")
        idle = sb("idle", [P, 1])
        power, power_ready = sb("power", [P, 2, NG * WI]), sem("power_ready")
        gn_rs, rs1_ready, rs2_ready = sem("gn_rs"), sem("rs1_ready"), sem("rs2_ready")
        csel = sb("csel", [P, 4])
        rank = sb("rank", [P, NT, E])
        top_step, ld_w, up_mm, h_ready, down_mm, added, out_done = (
            sem(n) for n in ("top_step", "ld_w", "up_mm", "h_ready", "down_mm", "added", "out_done"))

        block = ctx.enter_context(nc.Block())

        @block.sync
        def _(sp):
            sp.dma_start(t_row[:, :], t_d.rearrange("(a t) -> a t", a=1).broadcast_to([MIDCH, HT])).then_inc(ld_emb, 16)
            sp.dma_start(angles[:, :], c_angles_d).then_inc(ld_emb, 16)
            sp.dma_start(temb_rw[:, :], temb_rw_d).then_inc(ld_emb, 16)
            sp.dma_start(temb_iw[:, :], temb_iw_d).then_inc(ld_emb, 16)
            sp.dma_start(bias[:, :], bias_d).then_inc(ld_emb, 16)
            sp.dma_start(group[:, :], c_group_d).then_inc(ld_gn, 16)
            for c in range(4):
                n = TOK // 4
                sp.dma_start(xc[:, :, c * n:(c + 1) * n],
                             x_ch_d.rearrange("(h p) n -> p h n", p=P)[:, :, c * n:(c + 1) * n]).then_inc(ld_xc[c], 16)
            sp.dma_start(x[:, :, :], x_tok_d.rearrange("(n p) d -> p n d", p=P)).then_inc(ld_x, 16)
            with sp.Fori(0, E) as e:
                sp.wait_ge(down_mm, e * (4 * NTT) + 1)
                sp.dma_start(fc[:, :, :], w_fc_d[bass.ds(e, 1)].rearrange("a (h p) f -> p (a h) f", p=P)).then_inc(ld_w, 16)
                sp.dma_start(proj[:, :, :], w_proj_d[bass.ds(e, 1)].rearrange("a (c p) d -> p (a c) d", p=P)).then_inc(ld_w, 16)
            sp.wait_ge(added, E * NTT * 4 + 1)
            sp.dma_start(out_d.rearrange("(n p) d -> p n d", p=P), x[:, :, :]).then_inc(out_done, 16)
            sp.wait_ge(out_done, 16)

        @block.gpsimd
        def _(pool):
            nc.gpsimd.memset(power[:, 0, :], 0.5).then_inc(power_ready, 1)
            nc.gpsimd.memset(power[:, 1, :], -0.5).then_inc(power_ready, 1)
            pool.wait_ge(power_ready, 2)
            pool.wait_ge(ld_conv, 16 * 4)
            for src, dst, m in ((mixr_w, mix_r, 0), (mixi_w, mix_i, 1)):
                for g in range(NG):
                    nc.gpsimd.tensor_tensor(
                        dst[:, g], src[:, g].unsqueeze(2).broadcast_to([P, WI, MODES, 2]),
                        masks[:, m].rearrange("p (a x c) -> p a x c", a=1, c=2).broadcast_to([P, WI, MODES, 2]),
                        ALU.mult).then_inc(mix_built, 1)
            pool.wait_ge(wabs_step, 2)
            nc.gpsimd.tensor_tensor(wabs[:, :], wabs[:, :], power[:, 0, :], ALU.pow).then_inc(wabs_ready, 1)
            pool.wait_ge(wabs_ready, 1)
            for g in range(NG):
                nc.gpsimd.tensor_tensor(
                    mix_abs[:, g], wabs[:, g * WI:(g + 1) * WI].rearrange("p (o x c) -> p o x c", x=1, c=1).broadcast_to([P, WI, MODES, 2]),
                    masks[:, 2].rearrange("p (a x c) -> p a x c", a=1, c=2).broadcast_to([P, WI, MODES, 2]),
                    ALU.mult).then_inc(mix_built, 1)
            pool.wait_ge(temb_step, 4)
            nc.gpsimd.tensor_tensor(tabs[:, :], tabs[:, :], power[:, 0, 0:HT], ALU.pow).then_inc(temb_ready, 1)
            with pool.Fori(0, 4) as c:
                pool.wait_ge(gn_step, c * 7 + 7)
                nc.gpsimd.tensor_tensor(gtmp[:, 2, :], gtmp[:, 2, :], power[:, 1, 0:8], ALU.pow).then_inc(gn_rs, 1)

            def rsqrt(b, rs, step, ready):
                pool.wait_ge(step, b * 5 + 5)
                nc.gpsimd.tensor_tensor(rs[:, :], rs[:, :], power[:, 1, 0:2], ALU.pow).then_inc(ready, 1)

            def copy_spec(b):
                pool.wait_ge(idft_mm, b)
                nc.gpsimd.tensor_copy(spec_b[:, :], spec[:, bass.ds(b * SEQ, SEQ)]).then_inc(spec_copied, 1)

            ln1, ln2 = (rs1, ln1_step, rs1_ready), (rs2, ln2_step, rs2_ready)
            pool.wait_ge(spec_ready, WI)
            nc.gpsimd.tensor_copy(spec_b[:, :], spec[:, 0:SEQ]).then_inc(spec_copied, 1)
            copy_spec(1)
            rsqrt(0, *ln1)
            copy_spec(2)
            rsqrt(1, *ln1)
            with pool.Fori(2, B - 1) as k:
                copy_spec(k + 1)
                rsqrt(k, *ln1)
                rsqrt(k - 2, *ln2)
            rsqrt(B - 1, *ln1)
            rsqrt(B - 3, *ln2)
            rsqrt(B - 2, *ln2)
            rsqrt(B - 1, *ln2)

        @block.scalar
        def _(act):
            act.dma_start(mixr_w[:, :, :, :], mixr_w_d).then_inc(ld_conv, 16)
            act.dma_start(mixi_w[:, :, :, :], mixi_w_d).then_inc(ld_conv, 16)
            act.dma_start(masks[:, :, :], c_masks_d).then_inc(ld_conv, 16)
            act.dma_start(dft[:, :, :], c_dft_d.rearrange("(h p) m -> p h m", p=P)).then_inc(ld_conv, 16)
            for dst, src in ((wq, wq_d), (wk, wk_d), (wv, wv_d), (wo_t, wo_t_d)):
                act.dma_start(dst[:, :, :], src.rearrange("(h p) d -> p h d", p=P)).then_inc(ld_qkvo, 16)
            act.dma_start(ident[:, :], c_ident_d).then_inc(ld_attn, 16)
            act.dma_start(idft[:, :], c_idft_d).then_inc(ld_attn, 16)
            act.dma_start(causal[:, :], c_causal_d).then_inc(ld_attn, 16)
            act.dma_start(router[:, :, :], router_d.rearrange("(h p) e -> p h e", p=P)).then_inc(ld_attn, 16)
            act.wait_ge(emb_ready, 1)
            nc.scalar.activation(emb[:, :], ang[:, 0, :], ACT.Sin).then_inc(sin_ready, 1)
            for w, bank in ((qk_w, psG), (vo_w, psV)):
                act.wait_ge(qkvo_mm, 1 if w is qk_w else 2)
                nc.scalar.activation(w[:, :, :], bank[:, :], ACT.Copy).then_inc(qkvo_ready, 1)

            def front(b):
                act.wait_ge(t1_mm, b + 1)
                if not isinstance(b, int) or b > 0:
                    act.wait_ge(s_mm, b)
                nc.scalar.activation(xn_t[:, :, :], psT1[:, :], ACT.Copy).then_inc(xnt_ready, 1)
                act.wait_ge(g_mm, b + 1)
                nc.scalar.activation(g_t[:, :, :], psG[:, :], ACT.Copy, scale=float(D) ** -0.5).then_inc(gt_ready, 1)

            def values(b):
                act.wait_ge(v_mm, b + 1)
                if not isinstance(b, int) or b > 0:
                    act.wait_ge(pv_mm, b)
                nc.scalar.activation(v_b[:, :, :], psV[:, :], ACT.Copy).then_inc(v_ready, 1)

            def softmax(b):
                act.wait_ge(nmax_ready, b + 1)
                if not isinstance(b, int) or b > 0:
                    act.wait_ge(pt_mm, b)
                    act.wait_ge(rinv_ready, b)
                nc.scalar.activation(p_b[:, 0:P], s_b[:, 0:P], ACT.Exp, bias=nmax[:, 0:1],
                                     accum_out=rsum[:, 0:1]).then_inc(probs_ready, 1)
                nc.scalar.activation(p_b[:, P:3 * P], s_b[:, P:3 * P], ACT.Exp, bias=nmax[:, 1:2],
                                     accum_out=rsum[:, 1:2]).then_inc(probs_ready, 1)

            front(0)
            values(0)
            softmax(0)
            with act.Fori(1, B) as b:
                front(b)
                values(b)
                softmax(b)

            act.wait_ge(top_step, 13)
            nc.scalar.activation(top[:, 3, :], top[:, 2, :], ACT.Exp).then_inc(top_exp, 1)
            with act.Fori(0, E * NTT) as n:
                for f in range(FC):
                    act.wait_ge(up_mm, n * FC + f + 1)
                    if f == 0:
                        act.wait_ge(down_mm, n * 4 + 1)
                    nc.scalar.activation(h[:, f, :], banks[f % 4][:, :], ACT.Gelu).then_inc(h_ready, 1)

        @block.vector
        def _(dve):
            steps = [0]

            def link(ins):
                steps[0] += 1
                ins.then_inc(emb_step, 1)
                dve.wait_ge(emb_step, steps[0])

            v = nc.vector

            def alone(s, value):
                dve.wait_ge(s, value)
                v.memset(idle[:, :], 0.0)

            dve.wait_ge(ld_emb, 16 * 5)
            a, turns, near = ang[:, 0, :], ang[:, 1, :], ang[:, 2, :]
            link(v.tensor_scalar(a, t_row[:, :], angles[:, 0:1], None, ALU.mult))
            link(v.tensor_scalar(turns, a, 1 / TWO_PI, MAGIC, ALU.mult, ALU.add))
            link(v.tensor_scalar(turns, turns, MAGIC, None, ALU.subtract))
            for part in two_pi_parts():
                link(v.scalar_tensor_tensor(a, turns, -part, a, ALU.mult, ALU.add))
            link(v.tensor_scalar(a, a, PI_LOW, -PI_LOW, ALU.min, ALU.max))
            link(v.scalar_tensor_tensor(near, a, -1.0, a, ALU.mult, ALU.min))
            link(v.tensor_scalar(near, near, np.pi / 2, angles[:, 2:3], ALU.add, ALU.mult))
            v.scalar_tensor_tensor(a, a, angles[:, 1:2], near, ALU.mult, ALU.add).then_inc(emb_ready, 1)
            dve.wait_ge(ld_conv, 16 * 4)
            flat = mixr_w[:, :, :, :].rearrange("p g o c -> p (g o) c")
            v.tensor_tensor(sq[:, :, :], flat, flat, ALU.mult).then_inc(wabs_step, 1)
            dve.wait_ge(wabs_step, 1)
            v.tensor_tensor(wabs[:, :], sq[:, :, 0], sq[:, :, 1], ALU.add).then_inc(wabs_step, 1)
            dve.wait_ge(temb_mm, 1)
            for c in range(2):
                v.tensor_scalar(temb[:, c, :], psT1[:, c * HT:(c + 1) * HT], bias[:, c:c + 1], None,
                                ALU.add).then_inc(temb_step, 1)
            dve.wait_ge(temb_step, 2)
            v.tensor_tensor(tsq[:, :, :], temb[:, :, :], temb[:, :, :], ALU.mult).then_inc(temb_step, 1)
            dve.wait_ge(temb_step, 3)
            v.tensor_tensor(tabs[:, :], tsq[:, 0, :], tsq[:, 1, :], ALU.add).then_inc(temb_step, 1)
            dve.wait_ge(norm_mm, 1)
            v.tensor_scalar(inv[:, :], psI[:, 0:NG * HT], 1e-12, 1.0, ALU.add, ALU.max).then_inc(inv_step, 1)
            dve.wait_ge(inv_step, 1)
            v.reciprocal(inv[:, :], inv[:, :]).then_inc(inv_ready, 1)

            PER = 7
            for c in range(4):
                dve.wait_ge(ld_xc[c], 16)
                tiles = [(b, hh) for b in range(4) for hh in range(DH)]
                for j, (b, hh) in enumerate(tiles):
                    ins = v.bn_stats(gst[:, j, :], xc[:, hh, c * 1024 + b * SEQ:c * 1024 + (b + 1) * SEQ])
                ins.then_inc(gn_step, 1)
                dve.wait_ge(gn_step, c * PER + 1)
                for j in range(8):
                    ins = v.bn_aggr(gmv[:, j, :], gst[:, j, :])
                ins.then_inc(gn_step, 1)
                dve.wait_ge(gn_step, c * PER + 2)
                mean, var = gmv[:, :, 0], gmv[:, :, 1]
                v.tensor_tensor(gtmp[:, 0, :], mean, mean, ALU.mult).then_inc(gn_step, 1)
                dve.wait_ge(gn_step, c * PER + 3)
                v.tensor_tensor(var, var, gtmp[:, 0, :], ALU.add).then_inc(gn_stats, 1)
                dve.wait_ge(gn_mm, c + 1)
                v.tensor_copy(ggm[:, :, :], psT2[:, 0:16]).then_inc(gn_step, 1)
                dve.wait_ge(gn_step, c * PER + 4)
                v.tensor_tensor(gtmp[:, 1, :], ggm[:, :, 0], ggm[:, :, 0], ALU.mult).then_inc(gn_step, 1)
                dve.wait_ge(gn_step, c * PER + 5)
                v.tensor_tensor(gtmp[:, 2, :], ggm[:, :, 1], gtmp[:, 1, :], ALU.subtract).then_inc(gn_step, 1)
                dve.wait_ge(gn_step, c * PER + 6)
                v.tensor_scalar(gtmp[:, 2, :], gtmp[:, 2, :], GN_EPS, None, ALU.add).then_inc(gn_step, 1)
                dve.wait_ge(gn_rs, c + 1)
                for j, (b, hh) in enumerate(tiles):
                    at = xc[:, hh, c * 1024 + b * SEQ:c * 1024 + (b + 1) * SEQ]
                    v.tensor_scalar(at, at, ggm[:, j, 0:1], gtmp[:, 2, j:j + 1], ALU.subtract,
                                    ALU.mult).then_inc(gn_done, 1)
            dve.wait_ge(temb_ready, 1)
            for g in range(NG):
                dve.wait_ge(dft_mm, g + 1)
                for z, c in ((zr, 0), (zi, 1)):
                    v.tensor_tensor(z[:, g, :, :], banks[g][:, 0:B * HT],
                                    temb[:, c:c + 1, :].broadcast_to([P, B, HT]), ALU.mult).then_inc(z_ready, 1)
            dve.wait_ge(inv_ready, 1)
            for o in range(WI):
                og, j = o // 4, o % 4
                if j == 0:
                    dve.wait_ge(mix_mm, og + 1)
                rows = slice(32 * j, 32 * j + 32)
                v.tensor_tensor(spec[:, :].rearrange("p (b t o) -> p b t o", b=B, o=WI)[:, :, :, o],
                                banks[4 + og][rows, 0:B * HT],
                                inv[rows, og * HT:(og + 1) * HT].unsqueeze(1).broadcast_to([32, B, HT]),
                                ALU.mult).then_inc(spec_ready, 1)

            def norm(b, rows, st, mv, rs, outs, step, rs_ready, ready, read, first):
                for s in range(2):
                    v.bn_stats(st[:, s, :], rows[:, s, :]).then_inc(step, 1)
                alone(step, b * 5 + 2)
                for s in range(2):
                    v.bn_aggr(mv[:, s, :], st[:, s, :]).then_inc(step, 1)
                dve.wait_ge(step, b * 5 + 4)
                v.tensor_scalar(rs[:, :], mv[:, :, 1], LN_EPS, None, ALU.add).then_inc(step, 1)
                dve.wait_ge(rs_ready, b + 1)
                if not first:
                    dve.wait_ge(read, b)
                for s in range(2):
                    v.tensor_scalar(outs[:, s, :], rows[:, s, :], mv[:, s, 0:1], rs[:, s:s + 1],
                                    ALU.subtract, ALU.mult).then_inc(ready, 1)

            def tiles_of(b):
                return x[:, bass.ds(b * 2, 2), :]

            def conv_out(b, first=False):
                dve.wait_ge(idft_mm, b + 1)
                v.tensor_tensor(tiles_of(b), psI[:, :], tiles_of(b), ALU.add).then_inc(x1_ready, 1)
                alone(x1_ready, b + 1)
                norm(b, tiles_of(b), st1, mv1, rs1, xn, ln1_step, rs1_ready, xn_ready, t1_mm, first)

            def mask_and_max(b, first=False):
                dve.wait_ge(s_mm, b + 1)
                if not first:
                    dve.wait_ge(probs_ready, b * 2)
                v.tensor_tensor(s_b[:, 0:P], psS[:, 0:P], causal[:, P:2 * P], ALU.add).then_inc(s_masked, 1)
                v.tensor_tensor(s_b[:, P:3 * P], psS[:, P:3 * P], causal[:, :], ALU.add).then_inc(s_masked, 1)
                dve.wait_ge(s_masked, b * 2 + 2)
                v.tensor_reduce(nmax[:, 0:1], s_b[:, 0:P], AX_X, ALU.max, negate=True)
                v.tensor_reduce(nmax[:, 1:2], s_b[:, P:3 * P], AX_X, ALU.max, negate=True).then_inc(nmax_ready, 1)

            def probs_out(b):
                dve.wait_ge(pt_mm, b + 1)
                v.tensor_copy(p_t[:, :], psP[:, 0:3 * P]).then_inc(pt_ready, 1)
                dve.wait_ge(probs_ready, b * 2 + 2)
                v.reciprocal(rinv[:, :], rsum[:, :]).then_inc(rinv_ready, 1)

            def attn_out(b, first=False):
                dve.wait_ge(pv_mm, b + 1)
                dve.wait_ge(rinv_ready, b + 1)
                rows = tiles_of(b)
                for s in range(2):
                    v.scalar_tensor_tensor(rows[:, s, :], psO[:, s * D:(s + 1) * D], rinv[:, s:s + 1], rows[:, s, :],
                                           ALU.mult, ALU.add).then_inc(x2_ready, 1)
                alone(x2_ready, b * 2 + 2)
                norm(b, rows, st2, mv2, rs2, xn2, ln2_step, rs2_ready, xn2_ready, t2_mm, first)

            def router_in(b, first=False):
                dve.wait_ge(t2_mm, b + 1)
                if not first:
                    dve.wait_ge(r_mm, b)
                v.tensor_copy(xn2_t[:, :, :], psT2[:, :]).then_inc(xn2t_ready, 1)
                dve.wait_ge(xn2t_ready, b + 1)
                v.tensor_copy(xc[:, :, bass.ds(b * SEQ, SEQ)], xn2_t[:, :, :]).then_inc(xn2t_kept, 1)

            def logits_out(b):
                dve.wait_ge(r_mm, b + 1)
                v.tensor_copy(logits[:, bass.ds(b * 2, 2), :], psT2[:, 0:2 * E]).then_inc(logits_ready, 1)

            dve.wait_ge(ld_x, 16)
            dve.wait_ge(ld_attn, 16 * 4)
            conv_out(0, True)
            conv_out(1)
            mask_and_max(0, True)
            probs_out(0)
            conv_out(2)
            attn_out(0, True)
            mask_and_max(1)
            router_in(0, True)
            logits_out(0)
            probs_out(1)
            conv_out(3)
            attn_out(1)
            mask_and_max(2)
            with dve.Fori(3, B - 1) as k:
                router_in(k - 2)
                logits_out(k - 2)
                probs_out(k - 1)
                conv_out(k + 1)
                attn_out(k - 1)
                mask_and_max(k)
            router_in(B - 3)
            logits_out(B - 3)
            probs_out(B - 2)
            attn_out(B - 2)
            mask_and_max(B - 1)
            router_in(B - 2)
            logits_out(B - 2)
            probs_out(B - 1)
            attn_out(B - 1)
            router_in(B - 1)
            logits_out(B - 1)

            stp = [0]

            def then(ins):
                stp[0] += 1
                ins.then_inc(top_step, 1)
                dve.wait_ge(top_step, stp[0])

            dve.wait_ge(logits_ready, B)
            for e in range(E):
                ins = v.memset(rank[:, :, e], float(E - e))
            then(ins)

            def wide(a):
                return a.unsqueeze(2).broadcast_to([P, NT, E])

            l1 = logits[:, :, :]
            for n in range(2):
                best, key, one, cand = top[:, n, :], top[:, 2, :], hot[:, n], hot[:, 2]
                then(v.tensor_reduce(best, l1, AX_X, ALU.max))
                then(v.tensor_tensor(cand, l1, wide(best), ALU.is_equal))
                then(v.tensor_tensor(cand, cand, rank[:, :, :], ALU.mult))
                then(v.tensor_reduce(key, cand, AX_X, ALU.max))
                then(v.tensor_tensor(one, cand, wide(key), ALU.is_equal))
                if n == 0:
                    then(v.scalar_tensor_tensor(hot[:, 3], one, -3e38, l1, ALU.mult, ALU.add))
                    l1 = hot[:, 3]
            then(v.tensor_tensor(top[:, 2, :], top[:, 1, :], top[:, 0, :], ALU.subtract))
            dve.wait_ge(top_exp, 1)
            then(v.tensor_scalar(top[:, 0, :], top[:, 3, :], 1.0, None, ALU.add))
            then(v.reciprocal(top[:, 0, :], top[:, 0, :]))
            then(v.tensor_tensor(top[:, 1, :], top[:, 3, :], top[:, 0, :], ALU.mult))
            then(v.tensor_tensor(hot[:, 0], hot[:, 0], wide(top[:, 0, :]), ALU.mult))
            then(v.tensor_tensor(hot[:, 1], hot[:, 1], wide(top[:, 1, :]), ALU.mult))
            then(v.tensor_tensor(combine[:, :, :], hot[:, 0], hot[:, 1], ALU.add))
            with dve.Fori(0, E) as e:
                with dve.Fori(0, NTT) as m:
                    for s in range(4):
                        dve.wait_ge(down_mm, (e * NTT + m) * 4 + s + 2)
                        row = x[:, bass.ds(m * 4 + s, 1), :].rearrange("p a d -> p (a d)")
                        v.tensor_copy(csel[:, s:s + 1], combine[:, bass.ds(m * 4 + s, 1), bass.ds(e, 1)].rearrange("p a d -> p (a d)")).then_inc(csel_ready, 1)
                        dve.wait_ge(csel_ready, (e * NTT + m) * 4 + s + 1)
                        v.scalar_tensor_tensor(row, banks[4 + s][:, 0:D], csel[:, s:s + 1], row, ALU.mult, ALU.add).then_inc(added, 1)

        @block.tensor
        def _(pe):
            mm = nc.tensor.matmul
            pe.sem_inc(down_mm, 1)
            pe.sem_inc(added, 1)
            pe.wait_ge(ld_qkvo, 16 * 4)
            for w, m, bank in ((wq, wk, psG), (wv, wo_t, psV)):
                for a in range(DH):
                    for e in range(DH):
                        ins = mm(bank[:, a * D:(a + 1) * D], w[:, e, a * P:(a + 1) * P], m[:, e, :],
                                 start=(e == 0), stop=(e == DH - 1))
                ins.then_inc(qkvo_mm, 1)
            pe.wait_ge(ld_emb, 16 * 5)
            pe.wait_ge(sin_ready, 1)
            mm(psT1[:, 0:HT], temb_rw[:, :], emb[:, :], start=True, stop=True)
            mm(psT1[:, HT:2 * HT], temb_iw[:, :], emb[:, :], start=True, stop=True).then_inc(temb_mm, 1)
            pe.wait_ge(mix_built, 3 * NG)
            pe.wait_ge(temb_ready, 1)
            for og in range(NG):
                for g in range(NG):
                    ins = mm(psI[:, og * HT:(og + 1) * HT],
                             mix_abs[:, g, og * 4:(og + 1) * 4].rearrange("p o x c -> p (o x c)"), tabs[:, :],
                             start=(g == 0), stop=(g == NG - 1))
            ins.then_inc(norm_mm, 1)
            pe.wait_ge(ld_gn, 16)
            with pe.Fori(0, 4) as c:
                pe.wait_ge(gn_stats, c + 1)
                mm(psT2[:, 0:16], group[:, :], gmv[:, :, :], start=True, stop=True).then_inc(gn_mm, 1)
            pe.wait_ge(ld_conv, 16 * 4)
            pe.wait_ge(gn_done, NT)
            pe.wait_ge(qkvo_ready, 2)
            for g in range(NG):
                for j in range(4):
                    for hh in range(DH):
                        ins = mm(banks[g][32 * j:32 * j + 32, 0:B * HT], dft[:, hh, :],
                                 xc[:, hh, :].rearrange("p (n i) -> p i n", i=WI)[:, 4 * g + j, :],
                                 start=(hh == 0), stop=(hh == DH - 1))
                ins.then_inc(dft_mm, 1)
            pe.wait_ge(inv_ready, 1)
            for og in range(NG):
                for g in range(NG):
                    for n, (w, z) in enumerate(((mix_r, zr), (mix_i, zi))):
                        if og == 0:
                            pe.wait_ge(z_ready, 2 * g + n + 1)
                        ins = mm(banks[4 + og][:, 0:B * HT],
                                 w[:, g, og * 4:(og + 1) * 4].rearrange("p o x c -> p (o x c)"),
                                 z[:, g].rearrange("p b t -> p (b t)"), start=(g == 0 and n == 0),
                                 stop=(g == NG - 1 and n == 1))
                ins.then_inc(mix_mm, 1)

            pe.wait_ge(ld_attn, 16 * 4)

            def idft_of(b, first=False):
                pe.wait_ge(spec_copied, b + 1)
                if not first:
                    pe.wait_ge(x1_ready, b)
                for s in range(2):
                    ins = mm(psI[:, s * D:(s + 1) * D], spec_b[:, s * P:(s + 1) * P], idft[:, :], start=True, stop=True)
                ins.then_inc(idft_mm, 1)

            def transposes(b, rows, bank, ready, done, bank_read, first=False):
                pe.wait_ge(ready, b * 2 + 2)
                if not first:
                    pe.wait_ge(bank_read, b)
                for hh in range(DH):
                    for s in range(2):
                        ins = nc.tensor.transpose(bank[:, hh * SEQ + s * P:hh * SEQ + (s + 1) * P],
                                                  rows[:, s, hh * P:(hh + 1) * P], ident[:, :])
                ins.then_inc(done, 1)

            def project(b, first=False):
                pe.wait_ge(xnt_ready, b + 1)
                if not first:
                    pe.wait_ge(gt_ready, b)
                for a in range(DH):
                    for hh in range(DH):
                        ins = mm(psG[:, a * SEQ:(a + 1) * SEQ], qk_w[:, hh, a * P:(a + 1) * P], xn_t[:, hh, :],
                                 start=(hh == 0), stop=(hh == DH - 1))
                ins.then_inc(g_mm, 1)
                if not first:
                    pe.wait_ge(v_ready, b)
                for s in range(2):
                    for hh in range(DH):
                        ins = mm(psV[:, s * D:(s + 1) * D], xn_t[:, hh, s * P:(s + 1) * P], vo_w[:, hh, :],
                                 start=(hh == 0), stop=(hh == DH - 1))
                ins.then_inc(v_mm, 1)

            def route(b, first=False):
                pe.wait_ge(xn2t_ready, b + 1)
                for s in range(2):
                    for hh in range(DH):
                        ins = mm(psT2[:, s * E:(s + 1) * E], xn2_t[:, hh, s * P:(s + 1) * P],
                                 router[:, hh, :], start=(hh == 0), stop=(hh == DH - 1))
                ins.then_inc(r_mm, 1)

            def scores(b, first=False):
                pe.wait_ge(gt_ready, b + 1)
                if not first:
                    pe.wait_ge(s_masked, b * 2)
                for s in range(2):
                    for hh in range(DH):
                        ins = mm(psS[:, s * P:(2 * s + 1) * P], g_t[:, hh, s * P:(s + 1) * P],
                                 xn_t[:, hh, 0:(s + 1) * P], start=(hh == 0), stop=(hh == DH - 1))
                ins.then_inc(s_mm, 1)

            def probs_t(b, first=False):
                pe.wait_ge(probs_ready, b * 2 + 2)
                if not first:
                    pe.wait_ge(pt_ready, b)
                for n in range(3):
                    ins = nc.tensor.transpose(psP[:, n * P:(n + 1) * P], p_b[:, n * P:(n + 1) * P], ident[:, :])
                ins.then_inc(pt_mm, 1)

            def attend(b, first=False):
                pe.wait_ge(pt_ready, b + 1)
                pe.wait_ge(v_ready, b + 1)
                if not first:
                    pe.wait_ge(x2_ready, b * 2)
                mm(psO[:, 0:D], p_t[:, 0:P], v_b[:, 0, :], start=True, stop=True)
                mm(psO[:, D:2 * D], p_t[:, P:2 * P], v_b[:, 0, :], start=True, stop=False)
                mm(psO[:, D:2 * D], p_t[:, 2 * P:3 * P], v_b[:, 1, :], start=False, stop=True).then_inc(pv_mm, 1)

            t1 = (xn, psT1, xn_ready, t1_mm, xnt_ready)
            t2 = (xn2, psT2, xn2_ready, t2_mm, logits_ready)
            idft_of(0, True)
            transposes(0, *t1, True)
            project(0, True)
            idft_of(1)
            scores(0, True)
            transposes(1, *t1)
            project(1)
            probs_t(0, True)
            idft_of(2)
            attend(0, True)
            scores(1)
            transposes(2, *t1)
            transposes(0, *t2, True)
            project(2)
            route(0, True)
            probs_t(1)
            idft_of(3)
            attend(1)
            scores(2)
            with pe.Fori(3, B - 1) as k:
                transposes(k, *t1)
                transposes(k - 2, *t2)
                project(k)
                route(k - 2)
                probs_t(k - 1)
                idft_of(k + 1)
                attend(k - 1)
                scores(k)
            transposes(B - 1, *t1)
            transposes(B - 3, *t2)
            project(B - 1)
            route(B - 3)
            probs_t(B - 2)
            attend(B - 2)
            scores(B - 1)
            transposes(B - 2, *t2)
            route(B - 2)
            probs_t(B - 1)
            attend(B - 1)
            transposes(B - 1, *t2)
            route(B - 1)

            pe.wait_ge(logits_ready, B)
            pe.wait_ge(x2_ready, 2 * B)
            pe.wait_ge(xn2t_kept, B)
            with pe.Fori(0, E) as e:
                with pe.Fori(0, NTT) as m:
                    pe.wait_ge(ld_w, e * 32 + 32)
                    for f in range(FC):
                        if f >= 4:
                            pe.wait_ge(h_ready, (e * NTT + m) * FC + f - 3)
                        for hh in range(DH):
                            ins = mm(banks[f % 4][:, :], fc[:, hh, f * P:(f + 1) * P], xc[:, hh, bass.ds(m * TT, TT)],
                                     start=(hh == 0), stop=(hh == DH - 1))
                        ins.then_inc(up_mm, 1)
                    pe.wait_ge(h_ready, (e * NTT + m) * FC + FC)
                    for s in range(4):
                        pe.wait_ge(added, (e * NTT + m) * 4 + 1)
                        for f in range(FC):
                            ins = mm(banks[4 + s][:, 0:D], h[:, f, s * P:(s + 1) * P], proj[:, f, :],
                                     start=(f == 0), stop=(f == FC - 1))
                        ins.then_inc(down_mm, 1)


def laid_out(i):
    f = {n: np.asarray(a) for n, a in i.items()}
    flat = f["x"].reshape(TOK, D)
    w = f["L0_conv_weights1"]
    swapped = w[..., ::-1]
    mixr = np.stack([w, swapped], axis=3)
    mixi = np.stack([swapped, w], axis=3)

    def rows(a):
        return np.ascontiguousarray(a.transpose(0, 2, 3, 1, 4).reshape(NG, P, WI, 2).transpose(1, 0, 2, 3))

    ke = f["L0_conv_ke_weights"]
    temb_w = []
    for c in range(2):
        full = np.zeros((HEADS, MIDCH // HEADS, HEADS, MODES, 2), ke.dtype)
        for hd in range(HEADS):
            full[hd, :, hd] = ke[hd, :, c::2, None]
        temb_w.append(full.reshape(MIDCH, P))
    kb = f["L0_conv_ke_bias"].reshape(MODES, 2)
    bias = np.broadcast_to(kb[None, :, None, :], (4, MODES, 2, 2)).reshape(P, 2)
    return {
        "x_tok": flat, "x_ch": flat.T, "t": f["L0_conv_t"], "mixr_w": rows(mixr), "mixi_w": rows(mixi),
        "temb_rw": temb_w[0], "temb_iw": temb_w[1], "bias": bias, "wq": f["L1_attn_W_q"], "wk": f["L1_attn_W_k"],
        "wv": f["L1_attn_W_v"], "wo_t": f["L1_attn_W_o"].T, "router": f["L1_ffn_router_w"],
        "w_fc": f["L1_ffn_w_fc"], "w_proj": f["L1_ffn_w_proj"],
    }


def kernel(**inputs):
    import concourse.bacc as bacc
    from concourse.bass_utils import run_bass_kernel_spmd

    nc = bacc.Bacc("TRN2", target_bir_lowering=False, num_devices=1)
    arrays, args = {}, []
    for name, a in {**laid_out(inputs), **constants()}.items():
        a = np.ascontiguousarray(a)
        arrays["in_" + name] = a
        args.append(nc.dram_tensor("in_" + name, a.shape, mybir.dt.from_np(a.dtype), kind="ExternalInput").ap())
    args.append(nc.dram_tensor("out", (TOK, D), F32, kind="ExternalOutput").ap())
    hybrid_block(nc, *args)
    r = run_bass_kernel_spmd(nc, [arrays], core_ids=[0])
    return r.results[0]["out"].reshape(B, HT, WI, D)
```

```python
from contextlib import ExitStack

import numpy as np
import concourse.bass as bass
from concourse import mybir

F32 = mybir.dt.float32
F32R = mybir.dt.float32r
I32 = mybir.dt.int32
ALU = mybir.AluOpType
ACT = mybir.ActivationFunctionType
AX_X = mybir.AxisListType.X

P = 128
B, HT, WI, D = 16, 16, 16, 256
TOK = B * HT * WI
SEQ = HT * WI
NT = TOK // P
DH = D // P
MODES = 16
MC = 2 * MODES
NG = WI * MC // P
HEADS, MIDCH = 4, 32
GN_EPS, LN_EPS = 1e-5, 1e-5
E, DFF = 8, 1024
FC = DFF // P
PICKS = 2

GS = 256
GROUPS = (TOK * PICKS - E) // GS + E
ROW_W, ROW_ID = D, D + E
ROW = D + E + 1
REGION = TOK + GS
LATE = 3
IDLE_ROW = E * REGION

MASKED = -1e30
MAGIC = 1.5 * 2.0 ** 23
TWO_PI = 2.0 * np.pi
PI_LOW = 3.1415925


def two_pi_parts():
    parts, rest = [], TWO_PI
    for _ in range(3):
        step = 2.0 ** (np.floor(np.log2(rest)) - 8)
        parts.append(float(np.floor(rest / step) * step))
        rest -= parts[-1]
    return parts + [float(np.float32(rest))]


def constants():
    l = np.arange(D)
    x = np.arange(MODES)
    angle = 2 * np.pi * np.outer(l, x) / D
    dft = np.stack([np.cos(angle), -np.sin(angle)], axis=-1).reshape(D, MC)
    weight = np.where(x == 0, 1.0, 2.0)[:, None] / D
    idft = np.stack([np.cos(angle.T) * weight, -np.sin(angle.T) * weight], axis=1).reshape(MC, D)
    same_mode = np.repeat(np.repeat(np.eye(MODES), 2, 0), 2, 1)
    c, c2 = np.arange(MC)[:, None] % 2, np.arange(MC)[None, :] % 2
    sign_r = np.where((c == 1) & (c2 == 0), -1.0, 1.0)
    sign_i = np.where((c == 0) & (c2 == 1), 1.0, -1.0)
    masks = np.stack([same_mode * sign_r, same_mode * sign_i, same_mode * (c == 0)], axis=1)
    masks = np.tile(masks, (4, 1, 1))
    q, k = np.arange(P)[:, None], np.arange(P)[None, :]
    causal = np.concatenate([np.zeros((P, P)), np.where(k <= q, 0.0, MASKED)], axis=1)
    half = MIDCH // 2
    steps = -np.float32(np.log(10000.0)) * np.arange(half, dtype=np.float32) / np.float32(half)
    freqs = np.exp(steps.astype(np.float64)).astype(np.float32)
    angles = np.stack([np.tile(freqs, 2), np.repeat([1.0, 0.0], half), np.repeat([0.0, 1.0], half)], axis=1)
    f = np.float32
    fill = np.zeros((P, 2, ROW), np.float32)
    fill.view(np.int32)[:, :, ROW_ID] = TOK + np.arange(2)[None, :] * P + np.arange(P)[:, None]
    ids = (np.arange(NT)[None, :] * P + np.arange(P)[:, None]).astype(np.int32)
    experts = np.stack([np.tile(E - np.arange(E), (P, 2, 1)), np.tile(REGION * np.arange(E), (P, 2, 1))], axis=1)
    counting = np.stack([np.triu(np.ones((P, P)), 1), np.ones((P, P))], axis=1)
    numbers = np.broadcast_to(np.arange(GROUPS)[None, :, None], (P, GROUPS, E))
    return {
        "c_dft": dft.astype(f), "c_idft": idft.astype(f), "c_masks": masks.astype(f),
        "c_causal": causal.astype(f), "c_ident": np.eye(P, dtype=f),
        "c_group": np.kron(np.eye(P // 8), np.full((8, 8), 1 / 8)).astype(f),
        "c_angles": angles.astype(f), "c_fill": fill, "c_ids": ids, "c_experts": experts.astype(f),
        "c_counting": counting.astype(f), "c_numbers": numbers.astype(f),
    }


def hybrid_block(nc, x_tok_d, x_ch_d, t_d, mixr_w_d, mixi_w_d, temb_rw_d, temb_iw_d, bias_d, wq_d, wk_d, wv_d, wo_t_d,
                 router_d, w_ffn_d, c_dft_d, c_idft_d, c_masks_d, c_causal_d, c_ident_d, c_group_d,
                 c_angles_d, c_fill_d, c_ids_d, c_experts_d, c_counting_d, c_numbers_d, out_d, slots_d):
    with ExitStack() as ctx:
        start = -(-nc.sbuf_base // 32) * 32
        ctx.enter_context(nc.sbuf_tensor("arena", [P, nc.sbuf_usable_end - start - 64], mybir.dt.uint8))
        filled = {}

        def place(area, name, shape, dt=F32):
            at = filled.setdefault(area, AREAS[area][0])
            size = -(-int(np.prod(shape[1:])) * 4 // 32) * 32
            assert at + size <= AREAS[area][1], (area, name)
            filled[area] = at + size
            return nc.alloc_sbuf_tensor_at(name, shape, dt, offset=start + at)

        EXPERT = (DH * DFF + FC * D) * 4
        end = (nc.sbuf_usable_end - start - 64) // 32 * 32
        weights_at = end - E * EXPERT
        AREAS = {
            "always": (0, 2560),
            "ffn": (2560, weights_at),
            "weights": (weights_at, end),
            "attention": (2560, weights_at + LATE * EXPERT),
            "conv": (weights_at + LATE * EXPERT, end),
        }

        def at(name, shape, dt=F32):
            return place("attention", name, shape, dt)

        def cv(name, shape, dt=F32):
            return place("conv", name, shape, dt)

        def ff(name, shape, dt=F32):
            return place("ffn", name, shape, dt)

        def ps(name):
            return ctx.enter_context(nc.psum_tensor(name, [P, 512], F32))

        def sem(name):
            return ctx.enter_context(nc.semaphore(name))

        ident = place("always", "ident", [P, P])
        slot_w = place("always", "slot_w", [P, GROUPS, 2])
        slot_id = place("always", "slot_id", [P, GROUPS, 2], I32)
        table = place("always", "table", [P, 3, GROUPS], I32)
        add_id = place("always", "add_id", [P, 2], I32)

        xc = cv("xc", [P, DH, TOK])
        dft = cv("dft", [P, DH, MC])
        masks = cv("masks", [P, 3, MC])
        group = cv("group", [P, P])
        angles = cv("angles", [MIDCH, 3])
        wq, wk, wv, wo_t = (cv(n, [P, DH, D]) for n in ("wq", "wk", "wv", "wo_t"))
        mixr_w = cv("mixr_w", [P, NG, WI, 2])
        mixi_w = cv("mixi_w", [P, NG, WI, 2])
        mix_r = cv("mix_r", [P, NG, WI, MODES, 2])
        mix_i = cv("mix_i", [P, NG, WI, MODES, 2])
        mix_abs = cv("mix_abs", [P, NG, WI, MODES, 2])
        sq = cv("sq", [P, NG * WI, 2])
        wabs = cv("wabs", [P, NG * WI])
        temb_rw = cv("temb_rw", [MIDCH, P])
        temb_iw = cv("temb_iw", [MIDCH, P])
        bias = cv("bias", [P, 2])
        t_row = cv("t_row", [MIDCH, HT])
        ang = cv("ang", [MIDCH, 4, HT])
        emb = cv("emb", [MIDCH, HT])
        temb = cv("temb", [P, 2, HT])
        tsq = cv("tsq", [P, 2, HT])
        tabs = cv("tabs", [P, HT])
        inv = cv("inv", [P, NG * HT])
        gst = cv("gst", [P, 8, 6])
        gmv = cv("gmv", [P, 8, 2])
        ggm = cv("ggm", [P, 8, 2])
        gtmp = cv("gtmp", [P, 3, 8])
        zr = at("zr", [P, NG, B, HT])
        zi = at("zi", [P, NG, B, HT])

        x = at("x", [P, NT, D])
        power = at("power", [P, 2, NG * WI])
        causal = at("causal", [P, SEQ])
        idft = at("idft", [MC, D])
        router = at("router", [P, DH, E])
        experts = at("experts", [P, 2, 2, E])
        counting = at("counting", [P, 2, P])
        ids = at("ids", [P, NT], I32)
        fill = at("fill", [P, 2, ROW])
        spec = at("spec", [MC, TOK])
        qk_w = at("qk_w", [P, DH, D])
        vo_w = at("vo_w", [P, DH, D])
        spec_b = at("spec_b", [MC, SEQ])
        st1, st2 = at("st1", [P, 2, 6]), at("st2", [P, 2, 6])
        mv1, mv2 = at("mv1", [P, 2, 2]), at("mv2", [P, 2, 2])
        rs1, rs2 = at("rs1", [P, 2]), at("rs2", [P, 2])
        xn = at("xn", [P, 2, D])
        xn2 = at("xn2", [P, 2, D])
        xn2_kept = at("xn2_kept", [P, 2, D])
        row = at("row", [P, 2, ROW])
        xn_t = at("xn_t", [P, DH, SEQ])
        xn2_t = at("xn2_t", [P, DH, SEQ])
        g_t = at("g_t", [P, DH, SEQ])
        v_b = at("v_b", [P, 2, D])
        s_b = at("s_b", [P, 3 * P])
        p_b = at("p_b", [P, 3 * P])
        p_t = at("p_t", [P, 3 * P])
        nmax = at("nmax", [P, 2])
        rsum = at("rsum", [P, 2])
        rinv = at("rinv", [P, 2])
        logits = at("logits", [P, 2, E])
        hot = at("hot", [P, 2, 2, E])
        cand = at("cand", [P, 2, E])
        rest = at("rest", [P, 2, E])
        best = at("best", [P, 2, 2])
        key = at("key", [P, 2])
        gap = at("gap", [P, 2])
        ratio = at("ratio", [P, 2])
        pick_w = at("pick_w", [P, 2, 2])
        part = at("part", [P, 2, 2, E])
        weights = at("weights", [P, 2, E])
        picked = at("picked", [P, 2, E])
        before = at("before", [P, 2, E])
        where = at("where", [P, 2, E])
        slot_f = at("slot_f", [P, 2, 2])
        slot = at("slot", [P, 2, 2], I32)
        counts = at("counts", [P, 4, E])
        tail_f = at("tail_f", [P, E])
        tail = at("tail", [P, E], I32)
        numbers = at("numbers", [P, GROUPS, E])
        past = at("past", [P, GROUPS, E])
        past_end = at("past_end", [P, GROUPS, E])
        plan = at("plan", [P, 4, GROUPS])

        w_ffn = place("weights", "w_ffn", [P, E, DH * DFF + FC * D])
        fc_hi = [ff(f"fc_hi{n}", [P, DH, DFF], F32R) for n in range(2)]
        fc_lo = [ff(f"fc_lo{n}", [P, DH, DFF], F32R) for n in range(2)]
        pj_hi, pj_lo = (ff(n, [P, FC, D], F32R) for n in ("pj_hi", "pj_lo"))
        h_hi, h_lo = (ff(n, [P, FC, GS], F32R) for n in ("h_hi", "h_lo"))
        h = ff("h", [P, 2, 2, GS])
        xg = ff("xg", [P, 2, ROW])
        x_hi, x_lo = (ff(n, [P, DH, GS], F32R) for n in ("x_hi", "x_lo"))
        y = ff("y", [P, 2, D])

        psT1, psT2, psG, psV, psS, psP, psO, psI = banks = [ps(n) for n in (
            "psT1", "psT2", "psG", "psV", "psS", "psP", "psO", "psI")]
        ld_emb, ld_x, ld_qkvo, ld_gn, ld_conv, ld_attn = (
            sem(n) for n in ("ld_emb", "ld_x", "ld_qkvo", "ld_gn", "ld_conv", "ld_attn"))
        ld_xc = [sem(f"ld_xc{c}") for c in range(4)]
        emb_step, emb_ready, sin_ready, temb_mm, temb_step, temb_ready = (
            sem(n) for n in ("emb_step", "emb_ready", "sin_ready", "temb_mm", "temb_step", "temb_ready"))
        mix_built, wabs_step, wabs_ready, norm_mm, inv_step, inv_ready = (
            sem(n) for n in ("mix_built", "wabs_step", "wabs_ready", "norm_mm", "inv_step", "inv_ready"))
        qkvo_mm, qkvo_ready = sem("qkvo_mm"), sem("qkvo_ready")
        gn_step, gn_stats, gn_mm, gn_done = (sem(n) for n in ("gn_step", "gn_stats", "gn_mm", "gn_done"))
        dft_mm, z_ready, mix_mm, spec_ready = (sem(n) for n in ("dft_mm", "z_ready", "mix_mm", "spec_ready"))
        spec_copied, idft_mm, x1_ready, ln1_step, xn_ready = (
            sem(n) for n in ("spec_copied", "idft_mm", "x1_ready", "ln1_step", "xn_ready"))
        t1_mm, xnt_ready, g_mm, gt_ready, v_mm, v_ready, s_mm = (
            sem(n) for n in ("t1_mm", "xnt_ready", "g_mm", "gt_ready", "v_mm", "v_ready", "s_mm"))
        s_masked, nmax_ready, probs_ready, pt_mm, pt_ready, pv_mm, rinv_ready = (
            sem(n) for n in ("s_masked", "nmax_ready", "probs_ready", "pt_mm", "pt_ready", "pv_mm", "rinv_ready"))
        x2_ready, ln2_step, xn2_ready, t2_mm, xn2t_ready, r_mm = (
            sem(n) for n in ("x2_ready", "ln2_step", "xn2_ready", "t2_mm", "xn2t_ready", "r_mm"))
        gn_rs, rs1_ready, rs2_ready, power_ready = (sem(n) for n in ("gn_rs", "rs1_ready", "rs2_ready", "power_ready"))
        ld_route, ld_numbers, row_ready, pick_step, ones_ready = (
            sem(n) for n in ("ld_route", "ld_numbers", "row_ready", "pick_step", "ones_ready"))
        pool_passed, dve_passed, sp_passed = sem("pool_passed"), sem("dve_passed"), sem("sp_passed")
        kept, top_step, gap_ready, ratio_ready, weights_ready, picked_ready, before_ready = (
            sem(n) for n in ("kept", "top_step", "gap_ready", "ratio_ready", "weights_ready", "picked_ready", "before_ready"))
        where_mm, where_read, slot_step, slot_ready, row_filled, scattered, x2_stored = (
            sem(n) for n in ("where_mm", "where_read", "slot_step", "slot_ready", "row_filled", "scattered", "x2_stored"))
        counts_mm, plan_step, plan_ready, filled_up, idle_stored = (
            sem(n) for n in ("counts_mm", "plan_step", "plan_ready", "filled_up", "idle_stored"))
        ld_w = sem("ld_w")
        xg_loaded, xg_t_mm, x_hi_ready, x_lo_ready, meta_read, up_mm, gelu_done, h_hi_ready, h_ready = (
            sem(n) for n in ("xg_loaded", "xg_t_mm", "x_hi_ready", "x_lo_ready", "meta_read", "up_mm", "gelu_done", "h_hi_ready", "h_ready"))
        fc_hi_ready, fc_lo_ready, pj_hi_ready, pj_lo_ready, down_mm, y_ready, id_ready, y_added = (
            sem(n) for n in ("fc_hi_ready", "fc_lo_ready", "pj_hi_ready", "pj_lo_ready", "down_mm", "y_ready", "id_ready", "y_added"))

        def on(b):
            return not isinstance(b, int) or 0 <= b < B

        def later(b):
            return not isinstance(b, int) or b > 0

        def weights_in(eng, e):
            if e:
                eng.wait_ge(ld_w, 16 * e)
            eng.dma_start(w_ffn[:, E - 1 - e, :], w_ffn_d[e]).then_inc(ld_w, 16)

        def after_attention(eng):
            eng.wait_ge(x2_stored, 16 * (B + 1))
            eng.wait_ge(scattered, 16 * 2 * PICKS * B)
            eng.wait_ge(filled_up, 16 * E)
            eng.wait_ge(counts_mm, 1)
            eng.wait_ge(plan_ready, 2)

        def g_on(g):
            return not isinstance(g, int) or 0 <= g < GROUPS

        def run_groups(eng, body):
            body(0, 0)
            pairs = (GROUPS - 2) // 2
            with eng.Fori(0, pairs) as i:
                body(i * 2 + 1, 1)
                body(i * 2 + 2, 0)
            for g in range(1 + 2 * pairs, GROUPS):
                body(g, g % 2)

        FIRST_SLOTS, LOOP_SLOTS, LAST_SLOTS = range(0, 4), (4, B - 1), range(B - 1, B + 3)

        block = ctx.enter_context(nc.Block())

        @block.sync
        def _(sp):
            sp.dma_start(t_row[:, :], t_d.rearrange("(a t) -> a t", a=1).broadcast_to([MIDCH, HT])).then_inc(ld_emb, 16)
            sp.dma_start(angles[:, :], c_angles_d).then_inc(ld_emb, 16)
            sp.dma_start(temb_rw[:, :], temb_rw_d).then_inc(ld_emb, 16)
            sp.dma_start(temb_iw[:, :], temb_iw_d).then_inc(ld_emb, 16)
            sp.dma_start(bias[:, :], bias_d).then_inc(ld_emb, 16)
            sp.dma_start(group[:, :], c_group_d).then_inc(ld_gn, 16)
            for c in range(4):
                n = TOK // 4
                sp.dma_start(xc[:, :, c * n:(c + 1) * n],
                             x_ch_d.rearrange("(h p) n -> p h n", p=P)[:, :, c * n:(c + 1) * n]).then_inc(ld_xc[c], 16)
            sp.dma_start(x[:, :, :], x_tok_d.rearrange("(n p) d -> p n d", p=P)).then_inc(ld_x, 16)
            sp.wait_ge(ld_route, 16 * 4)
            sp.dma_start(slots_d[IDLE_ROW:IDLE_ROW + GS].rearrange("(s p) r -> p s r", p=P), fill[:, :, :]).then_inc(idle_stored, 16)
            sp.dma_start(out_d[TOK:TOK + GS].rearrange("(s p) d -> p s d", p=P), fill[:, :, 0:D]).then_inc(x2_stored, 16)

            sp.wait_ge(mix_mm, NG)
            sp.wait_ge(qkvo_mm, 2)
            sp.wait_ge(spec_ready, WI)
            for e in range(E - LATE):
                weights_in(sp, e)
            with sp.Fori(0, B) as b:
                sp.wait_ge(x2_ready, b * 2 + 2)
                sp.dma_start(out_d[bass.ds(b * SEQ, SEQ)].rearrange("(s p) d -> p s d", p=P),
                             x[:, bass.ds(b * 2, 2), :]).then_inc(x2_stored, 16)
            sp.wait_ge(plan_ready, 1)
            for e in range(E):
                at_row = sp.value_load(tail[0:1, e:e + 1], min_val=e * REGION, max_val=e * REGION + TOK)
                sp.dma_start(slots_d[bass.ds(at_row, GS)].rearrange("(s p) r -> p s r", p=P),
                             fill[:, :, :]).then_inc(filled_up, 16)
            def load_group(g):
                if later(g):
                    sp.wait_ge(meta_read, g * 2)
                    sp.wait_ge(xg_t_mm, g)
                    sp.sem_inc(sp_passed, 1)
                at_row = sp.value_load(table[0:1, 1, bass.ds(g, 1)], min_val=0, max_val=IDLE_ROW)
                sp.dma_start(xg[:, :, :], slots_d[bass.ds(at_row, GS)].rearrange("(s p) r -> p s r", p=P)).then_inc(xg_loaded, 16)

            after_attention(sp)
            sp.wait_ge(idle_stored, 16)
            for n in range(LATE):
                load_group(n)
                weights_in(sp, E - LATE + n)
            with sp.Fori(LATE, GROUPS) as g:
                load_group(g)
            sp.wait_ge(y_added, 32 * GROUPS)

        @block.gpsimd
        def _(pool):
            nc.gpsimd.memset(power[:, 0, :], 0.5).then_inc(power_ready, 1)
            nc.gpsimd.memset(power[:, 1, :], -0.5).then_inc(power_ready, 1)
            pool.wait_ge(power_ready, 2)
            pool.wait_ge(ld_conv, 16 * 4)
            for src, dst, m in ((mixr_w, mix_r, 0), (mixi_w, mix_i, 1)):
                for g in range(NG):
                    nc.gpsimd.tensor_tensor(
                        dst[:, g], src[:, g].unsqueeze(2).broadcast_to([P, WI, MODES, 2]),
                        masks[:, m].rearrange("p (a x c) -> p a x c", a=1, c=2).broadcast_to([P, WI, MODES, 2]),
                        ALU.mult).then_inc(mix_built, 1)
            pool.wait_ge(wabs_step, 2)
            nc.gpsimd.tensor_tensor(wabs[:, :], wabs[:, :], power[:, 0, :], ALU.pow).then_inc(wabs_ready, 1)
            pool.wait_ge(wabs_ready, 1)
            for g in range(NG):
                nc.gpsimd.tensor_tensor(
                    mix_abs[:, g], wabs[:, g * WI:(g + 1) * WI].rearrange("p (o x c) -> p o x c", x=1, c=1).broadcast_to([P, WI, MODES, 2]),
                    masks[:, 2].rearrange("p (a x c) -> p a x c", a=1, c=2).broadcast_to([P, WI, MODES, 2]),
                    ALU.mult).then_inc(mix_built, 1)
            pool.wait_ge(temb_step, 4)
            nc.gpsimd.tensor_tensor(tabs[:, :], tabs[:, :], power[:, 0, 0:HT], ALU.pow).then_inc(temb_ready, 1)
            with pool.Fori(0, 4) as c:
                pool.wait_ge(gn_step, c * 7 + 7)
                nc.gpsimd.tensor_tensor(gtmp[:, 2, :], gtmp[:, 2, :], power[:, 1, 0:8], ALU.pow).then_inc(gn_rs, 1)

            def gate():
                pool.sem_inc(pool_passed, 1)

            def rsqrt(b, rs, step, ready):
                pool.wait_ge(step, b * 5 + 5)
                nc.gpsimd.tensor_tensor(rs[:, :], rs[:, :], power[:, 1, 0:2], ALU.pow).then_inc(ready, 1)

            def copy_spec(b):
                pool.wait_ge(idft_mm, b)
                gate()
                nc.gpsimd.tensor_copy(spec_b[:, :], spec[:, bass.ds(b * SEQ, SEQ)]).then_inc(spec_copied, 1)

            def scatter(b):
                pool.wait_ge(row_filled, b + 1)
                pool.wait_ge(weights_ready, b + 1)
                gate()
                nc.gpsimd.tensor_copy(row[:, :, ROW_W:ROW_W + E], weights[:, :, :]).then_inc(row_ready, 1)
                nc.gpsimd.tensor_copy(row[:, :, ROW_ID].bitcast(I32), ids[:, bass.ds(b * 2, 2)]).then_inc(row_ready, 1)
                pool.wait_ge(row_ready, b * 2 + 2)
                pool.wait_ge(slot_ready, b + 1)
                gate()
                for s in range(2):
                    for n in range(PICKS):
                        nc.gpsimd.indirect_dma_start(
                            slots_d, bass.IndirectOffsetOnAxis(ap=slot[:, n, s:s + 1], axis=0), row[:, s, :],
                            None).then_inc(scattered, 16)

            def pool_slot(k):
                if on(k + 1):
                    if later(k + 1):
                        copy_spec(k + 1)
                    rsqrt(k + 1, rs1, ln1_step, rs1_ready)
                if on(k - 1):
                    rsqrt(k - 1, rs2, ln2_step, rs2_ready)
                if on(k - 3):
                    scatter(k - 3)

            pool.wait_ge(ld_route, 16 * 4)
            pool.wait_ge(spec_ready, WI)
            nc.gpsimd.tensor_copy(spec_b[:, :], spec[:, 0:SEQ]).then_inc(spec_copied, 1)
            pool_slot(-1)
            for k in FIRST_SLOTS:
                pool_slot(k)
            with pool.Fori(*LOOP_SLOTS) as k:
                pool_slot(k)
            for k in LAST_SLOTS:
                pool_slot(k)

            def add(g):
                if later(g):
                    pool.wait_ge(y_added, g * 32)
                pool.wait_ge(meta_read, g * 2 + 2)
                gate()
                nc.gpsimd.tensor_copy(add_id[:, :], slot_id[:, bass.ds(g, 1), :]).then_inc(id_ready, 1)
                pool.wait_ge(y_ready, g * 2 + 2)
                pool.wait_ge(id_ready, g + 1)
                gate()
                for s in range(2):
                    nc.gpsimd.indirect_dma_start(
                        out_d, bass.IndirectOffsetOnAxis(ap=add_id[:, s:s + 1], axis=0), y[:, s, :], None,
                        compute_op=ALU.add).then_inc(y_added, 16)

            def proj_lower(g):
                e = pool.value_load(table[0:1, 0, bass.ds(g, 1)], min_val=0, max_val=E - 1)
                for a in range(2):
                    pool.wait_ge(pj_hi_ready, g * 2 + a + 1)
                    nc.gpsimd.tensor_tensor(
                        pj_lo[:, 4 * a:4 * a + 4, :],
                        w_ffn[:, bass.ds(e, 1), (2 + a) * DFF:(3 + a) * DFF].rearrange("p a (c d) -> p (a c) d", d=D),
                        pj_hi[:, 4 * a:4 * a + 4, :].bitcast(F32), ALU.subtract).then_inc(pj_lo_ready, 1)

            after_attention(pool)
            pool.sem_inc(pool_passed, 1)
            proj_lower(0)
            proj_lower(1)
            add(0)
            with pool.Fori(2, GROUPS) as g:
                proj_lower(g)
                add(g - 1)
            add(GROUPS - 1)

        @block.scalar
        def _(act):
            act.dma_start(mixr_w[:, :, :, :], mixr_w_d).then_inc(ld_conv, 16)
            act.dma_start(mixi_w[:, :, :, :], mixi_w_d).then_inc(ld_conv, 16)
            act.dma_start(masks[:, :, :], c_masks_d).then_inc(ld_conv, 16)
            act.dma_start(dft[:, :, :], c_dft_d.rearrange("(h p) m -> p h m", p=P)).then_inc(ld_conv, 16)
            for dst, src in ((wq, wq_d), (wk, wk_d), (wv, wv_d), (wo_t, wo_t_d)):
                act.dma_start(dst[:, :, :], src.rearrange("(h p) d -> p h d", p=P)).then_inc(ld_qkvo, 16)
            act.dma_start(ident[:, :], c_ident_d).then_inc(ld_attn, 16)
            act.dma_start(idft[:, :], c_idft_d).then_inc(ld_attn, 16)
            act.dma_start(causal[:, :], c_causal_d).then_inc(ld_attn, 16)
            act.dma_start(router[:, :, :], router_d.rearrange("(h p) e -> p h e", p=P)).then_inc(ld_attn, 16)
            for dst, src in ((experts[:, :, :, :], c_experts_d), (counting[:, :, :], c_counting_d), (ids[:, :], c_ids_d),
                             (fill[:, :, :], c_fill_d)):
                act.dma_start(dst, src).then_inc(ld_route, 16)
            act.dma_start(numbers[:, :, :], c_numbers_d).then_inc(ld_numbers, 16)
            act.wait_ge(emb_ready, 1)
            nc.scalar.activation(emb[:, :], ang[:, 0, :], ACT.Sin).then_inc(sin_ready, 1)
            for w, bank in ((qk_w, psG), (vo_w, psV)):
                act.wait_ge(qkvo_mm, 1 if w is qk_w else 2)
                nc.scalar.activation(w[:, :, :], bank[:, :], ACT.Copy).then_inc(qkvo_ready, 1)

            def copy(out, src, done, **kw):
                nc.scalar.activation(out, src, ACT.Copy, **kw).then_inc(done, 1)

            def front(b):
                act.wait_ge(t1_mm, b + 1)
                if later(b):
                    act.wait_ge(s_mm, b)
                copy(xn_t[:, :, :], psT1[:, :], xnt_ready)
                act.wait_ge(g_mm, b + 1)
                copy(g_t[:, :, :], psG[:, :], gt_ready, scale=float(D) ** -0.5)

            def router_in(b):
                act.wait_ge(t2_mm, b + 1)
                if later(b):
                    act.wait_ge(r_mm, b)
                copy(xn2_t[:, :, :], psT2[:, :], xn2t_ready)
                if later(b):
                    act.wait_ge(row_filled, b)
                copy(xn2_kept[:, :, :], xn2[:, :, :], kept)

            def probs_out(b):
                act.wait_ge(pt_mm, b + 1)
                if later(b):
                    act.wait_ge(pv_mm, b)
                copy(p_t[:, :], psP[:, 0:3 * P], pt_ready)

            def values(b):
                act.wait_ge(v_mm, b + 1)
                if later(b):
                    act.wait_ge(pv_mm, b)
                copy(v_b[:, :, :], psV[:, :], v_ready)

            def pick_ratio(b):
                act.wait_ge(gap_ready, b + 1)
                if later(b):
                    act.wait_ge(weights_ready, b)
                nc.scalar.activation(ratio[:, :], gap[:, :], ACT.Exp).then_inc(ratio_ready, 1)

            def fill_row(b):
                act.wait_ge(kept, b + 1)
                if later(b):
                    act.wait_ge(scattered, b * (16 * 2 * PICKS))
                copy(row[:, :, 0:D], xn2_kept[:, :, :], row_filled)

            def softmax(b):
                act.wait_ge(nmax_ready, b + 1)
                if later(b):
                    act.wait_ge(pt_mm, b)
                    act.wait_ge(rinv_ready, b)
                nc.scalar.activation(p_b[:, 0:P], s_b[:, 0:P], ACT.Exp, bias=nmax[:, 0:1],
                                     accum_out=rsum[:, 0:1]).then_inc(probs_ready, 1)
                nc.scalar.activation(p_b[:, P:3 * P], s_b[:, P:3 * P], ACT.Exp, bias=nmax[:, 1:2],
                                     accum_out=rsum[:, 1:2]).then_inc(probs_ready, 1)

            def act_slot(k):
                if on(k):
                    front(k)
                if on(k - 3):
                    pick_ratio(k - 3)
                    fill_row(k - 3)
                if on(k - 2):
                    router_in(k - 2)
                if on(k - 1):
                    probs_out(k - 1)
                if on(k):
                    values(k)
                    softmax(k)

            for k in FIRST_SLOTS:
                act_slot(k)
            with act.Fori(*LOOP_SLOTS) as k:
                act_slot(k)
            for k in LAST_SLOTS:
                act_slot(k)

            def expert_of(g):
                return act.value_load(table[0:1, 0, bass.ds(g, 1)], min_val=0, max_val=E - 1)

            def fc_upper(g, par):
                e = expert_of(g)
                landed = act.value_load(table[0:1, 2, bass.ds(g, 1)], min_val=16, max_val=16 * E)
                if not isinstance(g, int) or g > 1:
                    act.wait_ge(up_mm, g * 4 - 4)
                act.wait_ge(ld_w, landed)
                for a in range(DH):
                    copy(fc_hi[par][:, a, :], w_ffn[:, bass.ds(e, 1), a * DFF:(a + 1) * DFF].rearrange("p a f -> p (a f)"),
                         fc_hi_ready)

            def proj_upper(g, a):
                e = expert_of(g)
                if later(g):
                    act.wait_ge(down_mm, g * 2 + a - 1)
                copy(pj_hi[:, 4 * a:4 * a + 4, :],
                     w_ffn[:, bass.ds(e, 1), (2 + a) * DFF:(3 + a) * DFF].rearrange("p a (c d) -> p (a c) d", d=D),
                     pj_hi_ready)

            def x_upper(g):
                act.wait_ge(xg_t_mm, g + 1)
                if later(g):
                    act.wait_ge(up_mm, g * 4)
                copy(x_hi[:, :, :], psS[:, :], x_hi_ready)

            def gelu(g, c):
                act.wait_ge(up_mm, g * 4 + c + 1)
                if c >= 2 or later(g):
                    act.wait_ge(h_ready, g * 4 + c - 1)
                nc.scalar.activation(h[:, c % 2, :, :], banks[c][:, :], ACT.Gelu).then_inc(gelu_done, 1)

            def outputs(g):
                act.wait_ge(down_mm, g * 2 + 2)
                if later(g):
                    act.wait_ge(y_added, g * 32)
                for s, bank in enumerate((psP, psO)):
                    nc.scalar.activation(y[:, s, :], bank[:, 0:D], ACT.Copy,
                                         scale=slot_w[:, bass.ds(g, 1), s]).then_inc(y_ready, 1)

            def act_group(g, par):
                gelu(g, 0)
                proj_upper(g, 1)
                gelu(g, 1)
                if g_on(g - 1):
                    outputs(g - 1)
                gelu(g, 2)
                gelu(g, 3)
                if g_on(g + 1):
                    x_upper(g + 1)
                    fc_upper(g + 1, 1 - par)
                    proj_upper(g + 1, 0)

            after_attention(act)
            fc_upper(0, 0)
            x_upper(0)
            proj_upper(0, 0)
            run_groups(act, act_group)
            outputs(GROUPS - 1)

        @block.vector
        def _(dve):
            steps = [0]

            def link(ins):
                steps[0] += 1
                ins.then_inc(emb_step, 1)
                dve.wait_ge(emb_step, steps[0])

            v = nc.vector

            def alone(s, value):
                dve.wait_ge(s, value)
                dve.sem_inc(dve_passed, 1)

            dve.wait_ge(ld_emb, 16 * 5)
            a, turns, near = ang[:, 0, :], ang[:, 1, :], ang[:, 2, :]
            link(v.tensor_scalar(a, t_row[:, :], angles[:, 0:1], None, ALU.mult))
            link(v.tensor_scalar(turns, a, 1 / TWO_PI, MAGIC, ALU.mult, ALU.add))
            link(v.tensor_scalar(turns, turns, MAGIC, None, ALU.subtract))
            for turn in two_pi_parts():
                link(v.scalar_tensor_tensor(a, turns, -turn, a, ALU.mult, ALU.add))
            link(v.tensor_scalar(a, a, PI_LOW, -PI_LOW, ALU.min, ALU.max))
            link(v.scalar_tensor_tensor(near, a, -1.0, a, ALU.mult, ALU.min))
            link(v.tensor_scalar(near, near, np.pi / 2, angles[:, 2:3], ALU.add, ALU.mult))
            v.scalar_tensor_tensor(a, a, angles[:, 1:2], near, ALU.mult, ALU.add).then_inc(emb_ready, 1)
            dve.wait_ge(ld_conv, 16 * 4)
            flat = mixr_w[:, :, :, :].rearrange("p g o c -> p (g o) c")
            v.tensor_tensor(sq[:, :, :], flat, flat, ALU.mult).then_inc(wabs_step, 1)
            dve.wait_ge(wabs_step, 1)
            v.tensor_tensor(wabs[:, :], sq[:, :, 0], sq[:, :, 1], ALU.add).then_inc(wabs_step, 1)
            dve.wait_ge(temb_mm, 1)
            for c in range(2):
                v.tensor_scalar(temb[:, c, :], psT1[:, c * HT:(c + 1) * HT], bias[:, c:c + 1], None,
                                ALU.add).then_inc(temb_step, 1)
            dve.wait_ge(temb_step, 2)
            v.tensor_tensor(tsq[:, :, :], temb[:, :, :], temb[:, :, :], ALU.mult).then_inc(temb_step, 1)
            dve.wait_ge(temb_step, 3)
            v.tensor_tensor(tabs[:, :], tsq[:, 0, :], tsq[:, 1, :], ALU.add).then_inc(temb_step, 1)
            dve.wait_ge(norm_mm, 1)
            v.tensor_scalar(inv[:, :], psI[:, 0:NG * HT], 1e-12, 1.0, ALU.add, ALU.max).then_inc(inv_step, 1)
            dve.wait_ge(inv_step, 1)
            v.reciprocal(inv[:, :], inv[:, :]).then_inc(inv_ready, 1)

            PER = 7
            for c in range(4):
                dve.wait_ge(ld_xc[c], 16)
                tiles = [(b, hh) for b in range(4) for hh in range(DH)]
                for j, (b, hh) in enumerate(tiles):
                    ins = v.bn_stats(gst[:, j, :], xc[:, hh, c * 1024 + b * SEQ:c * 1024 + (b + 1) * SEQ])
                ins.then_inc(gn_step, 1)
                dve.wait_ge(gn_step, c * PER + 1)
                for j in range(8):
                    ins = v.bn_aggr(gmv[:, j, :], gst[:, j, :])
                ins.then_inc(gn_step, 1)
                dve.wait_ge(gn_step, c * PER + 2)
                mean, var = gmv[:, :, 0], gmv[:, :, 1]
                v.tensor_tensor(gtmp[:, 0, :], mean, mean, ALU.mult).then_inc(gn_step, 1)
                dve.wait_ge(gn_step, c * PER + 3)
                v.tensor_tensor(var, var, gtmp[:, 0, :], ALU.add).then_inc(gn_stats, 1)
                dve.wait_ge(gn_mm, c + 1)
                v.tensor_copy(ggm[:, :, :], psT2[:, 0:16]).then_inc(gn_step, 1)
                dve.wait_ge(gn_step, c * PER + 4)
                v.tensor_tensor(gtmp[:, 1, :], ggm[:, :, 0], ggm[:, :, 0], ALU.mult).then_inc(gn_step, 1)
                dve.wait_ge(gn_step, c * PER + 5)
                v.tensor_tensor(gtmp[:, 2, :], ggm[:, :, 1], gtmp[:, 1, :], ALU.subtract).then_inc(gn_step, 1)
                dve.wait_ge(gn_step, c * PER + 6)
                v.tensor_scalar(gtmp[:, 2, :], gtmp[:, 2, :], GN_EPS, None, ALU.add).then_inc(gn_step, 1)
                dve.wait_ge(gn_rs, c + 1)
                for j, (b, hh) in enumerate(tiles):
                    at = xc[:, hh, c * 1024 + b * SEQ:c * 1024 + (b + 1) * SEQ]
                    v.tensor_scalar(at, at, ggm[:, j, 0:1], gtmp[:, 2, j:j + 1], ALU.subtract,
                                    ALU.mult).then_inc(gn_done, 1)
            dve.wait_ge(temb_ready, 1)
            for g in range(NG):
                dve.wait_ge(dft_mm, g + 1)
                for z, c in ((zr, 0), (zi, 1)):
                    v.tensor_tensor(z[:, g, :, :], banks[g][:, 0:B * HT],
                                    temb[:, c:c + 1, :].broadcast_to([P, B, HT]), ALU.mult).then_inc(z_ready, 1)
            dve.wait_ge(inv_ready, 1)
            for o in range(WI):
                og, j = o // 4, o % 4
                if j == 0:
                    dve.wait_ge(mix_mm, og + 1)
                rows = slice(32 * j, 32 * j + 32)
                v.tensor_tensor(spec[:, :].rearrange("p (b t o) -> p b t o", b=B, o=WI)[:, :, :, o],
                                banks[4 + og][rows, 0:B * HT],
                                inv[rows, og * HT:(og + 1) * HT].unsqueeze(1).broadcast_to([32, B, HT]),
                                ALU.mult).then_inc(spec_ready, 1)

            def norm(b, rows, st, mv, rs, outs, step, rs_ready, ready, read, read_too=None):
                for s in range(2):
                    v.bn_stats(st[:, s, :], rows[:, s, :]).then_inc(step, 1)
                alone(step, b * 5 + 2)
                for s in range(2):
                    v.bn_aggr(mv[:, s, :], st[:, s, :]).then_inc(step, 1)
                dve.wait_ge(step, b * 5 + 4)
                v.tensor_scalar(rs[:, :], mv[:, :, 1], LN_EPS, None, ALU.add).then_inc(step, 1)
                dve.wait_ge(rs_ready, b + 1)
                if later(b):
                    dve.wait_ge(read, b)
                    if read_too is not None:
                        dve.wait_ge(read_too, b)
                for s in range(2):
                    v.tensor_scalar(outs[:, s, :], rows[:, s, :], mv[:, s, 0:1], rs[:, s:s + 1],
                                    ALU.subtract, ALU.mult).then_inc(ready, 1)

            def tiles_of(b):
                return x[:, bass.ds(b * 2, 2), :]

            def conv_out(b):
                dve.wait_ge(idft_mm, b + 1)
                v.tensor_tensor(tiles_of(b), psI[:, :], tiles_of(b), ALU.add).then_inc(x1_ready, 1)
                alone(x1_ready, b + 1)
                norm(b, tiles_of(b), st1, mv1, rs1, xn, ln1_step, rs1_ready, xn_ready, t1_mm)

            def mask_and_max(b):
                dve.wait_ge(s_mm, b + 1)
                if later(b):
                    dve.wait_ge(probs_ready, b * 2)
                v.tensor_tensor(s_b[:, 0:P], psS[:, 0:P], causal[:, P:2 * P], ALU.add).then_inc(s_masked, 1)
                v.tensor_tensor(s_b[:, P:3 * P], psS[:, P:3 * P], causal[:, :], ALU.add).then_inc(s_masked, 1)
                dve.wait_ge(s_masked, b * 2 + 2)
                v.tensor_reduce(nmax[:, 0:1], s_b[:, 0:P], AX_X, ALU.max, negate=True)
                v.tensor_reduce(nmax[:, 1:2], s_b[:, P:3 * P], AX_X, ALU.max, negate=True).then_inc(nmax_ready, 1)

            def attn_out(b):
                dve.wait_ge(probs_ready, b * 2 + 2)
                v.reciprocal(rinv[:, :], rsum[:, :]).then_inc(rinv_ready, 1)
                dve.wait_ge(pv_mm, b + 1)
                dve.wait_ge(rinv_ready, b + 1)
                rows = tiles_of(b)
                for s in range(2):
                    v.scalar_tensor_tensor(rows[:, s, :], psO[:, s * D:(s + 1) * D], rinv[:, s:s + 1], rows[:, s, :],
                                           ALU.mult, ALU.add).then_inc(x2_ready, 1)
                alone(x2_ready, b * 2 + 2)
                norm(b, rows, st2, mv2, rs2, xn2, ln2_step, rs2_ready, xn2_ready, t2_mm, kept)

            def wide(a):
                return a.unsqueeze(2).broadcast_to([P, 2, E])

            def pick(b):
                STEPS = 15
                count = [0]

                def then(ins):
                    count[0] += 1
                    ins.then_inc(top_step, 1)
                    dve.wait_ge(top_step, b * STEPS + count[0])

                dve.wait_ge(r_mm, b + 1)
                then(v.tensor_copy(logits[:, :, :], psT2[:, 0:2 * E]))
                left = logits[:, :, :]
                for n in range(PICKS):
                    then(v.tensor_reduce(best[:, n, :], left, AX_X, ALU.max))
                    then(v.tensor_tensor(cand[:, :, :], left, wide(best[:, n, :]), ALU.is_equal))
                    then(v.tensor_tensor(cand[:, :, :], cand[:, :, :], experts[:, 0], ALU.mult))
                    then(v.tensor_reduce(key[:, :], cand[:, :, :], AX_X, ALU.max))
                    then(v.tensor_tensor(hot[:, n], cand[:, :, :], wide(key[:, :]), ALU.is_equal))
                    if n == 0:
                        then(v.scalar_tensor_tensor(rest[:, :, :], hot[:, 0], -3e38, left, ALU.mult, ALU.add))
                        left = rest[:, :, :]
                v.tensor_tensor(gap[:, :], best[:, 1, :], best[:, 0, :], ALU.subtract).then_inc(gap_ready, 1)
                if later(b):
                    dve.wait_ge(before_ready, b)
                    dve.wait_ge(where_mm, b)
                    v.tensor_tensor(before[:, 0], before[:, 1], picked[:, 1], ALU.add).then_inc(before_ready, 1)
                    dve.wait_ge(before_ready, b * 2 + 1)
                else:
                    v.memset(before[:, 0], 0.0).then_inc(before_ready, 1)
                    dve.wait_ge(before_ready, 1)
                then(v.tensor_tensor(picked[:, :, :], hot[:, 0], hot[:, 1], ALU.add))
                v.tensor_tensor(before[:, 1], before[:, 0], picked[:, 0], ALU.add).then_inc(before_ready, 1)
                dve.wait_ge(ratio_ready, b + 1)
                then(v.tensor_scalar(pick_w[:, 0, :], ratio[:, :], 1.0, None, ALU.add))
                then(v.reciprocal(pick_w[:, 0, :], pick_w[:, 0, :]))
                v.tensor_tensor(pick_w[:, 1, :], ratio[:, :], pick_w[:, 0, :], ALU.mult).then_inc(pick_step, 1)
                v.tensor_tensor(part[:, 0], hot[:, 0], wide(pick_w[:, 0, :]), ALU.mult).then_inc(pick_step, 1)
                dve.wait_ge(pick_step, b * 3 + 2)
                v.tensor_tensor(part[:, 1], hot[:, 1], wide(pick_w[:, 1, :]), ALU.mult).then_inc(pick_step, 1)
                dve.wait_ge(pick_step, b * 3 + 3)
                if later(b):
                    dve.wait_ge(row_ready, b * 2)
                v.tensor_tensor(weights[:, :, :], part[:, 0], part[:, 1], ALU.add).then_inc(weights_ready, 1)
                assert count[0] == STEPS

            def find_slots(b):
                dve.wait_ge(where_mm, b + 1)
                v.tensor_tensor(where[:, :, :], psS[:, 0:2 * E], experts[:, 1], ALU.add).then_inc(where_read, 1)
                dve.wait_ge(where_read, b + 1)
                for n in range(PICKS):
                    v.tensor_tensor(part[:, n], hot[:, n], where[:, :, :], ALU.mult).then_inc(slot_step, 1)
                dve.wait_ge(slot_step, b * 3 + 2)
                v.tensor_reduce(slot_f[:, :, :], part[:, :, :, :], AX_X, ALU.add).then_inc(slot_step, 1)
                dve.wait_ge(slot_step, b * 3 + 3)
                if later(b):
                    dve.wait_ge(scattered, b * (16 * 2 * PICKS))
                v.tensor_copy(slot[:, :, :], slot_f[:, :, :]).then_inc(slot_ready, 1)

            def dve_slot(k):
                if on(k - 3):
                    pick(k - 3)
                if on(k + 1):
                    conv_out(k + 1)
                if on(k - 3):
                    find_slots(k - 3)
                if on(k - 1):
                    attn_out(k - 1)
                if on(k):
                    mask_and_max(k)

            dve.wait_ge(ld_x, 16)
            dve.wait_ge(ld_attn, 16 * 4)
            dve.wait_ge(ld_route, 16 * 4)
            conv_out(0)
            for k in FIRST_SLOTS:
                dve_slot(k)
            with dve.Fori(*LOOP_SLOTS) as k:
                dve_slot(k)
            for k in LAST_SLOTS:
                dve_slot(k)

            plan_steps = [0]

            def step(ins):
                plan_steps[0] += 1
                ins.then_inc(plan_step, 1)
                dve.wait_ge(plan_step, plan_steps[0])

            n_slots, n_groups, ends, ones = counts[:, 0], counts[:, 1], counts[:, 2], counts[:, 3]
            step(v.tensor_tensor(before[:, 0], before[:, 1], picked[:, 1], ALU.add))
            v.memset(ones, 1.0).then_inc(ones_ready, 1)
            dve.wait_ge(ones_ready, 1)
            dve.wait_ge(counts_mm, 1)
            step(v.tensor_copy(n_slots, psS[:, 0:E]))
            step(v.tensor_tensor(tail_f[:, :], n_slots, experts[:, 1, 0, :], ALU.add))
            v.tensor_copy(tail[:, :], tail_f[:, :]).then_inc(plan_ready, 1)
            step(v.tensor_scalar(n_groups, n_slots, 1.0 / GS, 127.5 / GS, ALU.mult, ALU.add))
            step(v.tensor_scalar(n_groups, n_groups, MAGIC, None, ALU.add))
            step(v.tensor_scalar(n_groups, n_groups, MAGIC, None, ALU.subtract))
            step(v.tensor_tensor_scan(ends, ones, n_groups, 0.0, ALU.mult, ALU.add))
            dve.wait_ge(ld_numbers, 16)
            all_ends = ends.unsqueeze(1).broadcast_to([P, GROUPS, E])
            step(v.tensor_tensor(past[:, :, :], numbers[:, :, :], all_ends, ALU.is_ge))
            step(v.tensor_tensor(past_end[:, :, :], past[:, :, :], all_ends, ALU.mult))
            step(v.tensor_reduce(plan[:, 0, :], past[:, :, :], AX_X, ALU.add))
            step(v.tensor_reduce(plan[:, 1, :], past_end[:, :, :], AX_X, ALU.max))
            step(v.tensor_tensor(plan[:, 1, :], numbers[:, :, 0], plan[:, 1, :], ALU.subtract))
            step(v.tensor_scalar(plan[:, 2, :], plan[:, 0, :], float(E), float(GS), ALU.is_lt, ALU.mult))
            step(v.tensor_tensor(plan[:, 1, :], plan[:, 1, :], plan[:, 2, :], ALU.mult))
            step(v.scalar_tensor_tensor(plan[:, 1, :], plan[:, 0, :], float(REGION), plan[:, 1, :], ALU.mult, ALU.add))
            step(v.tensor_copy(table[:, 1, :], plan[:, 1, :]))
            step(v.tensor_scalar(plan[:, 3, :], plan[:, 0, :], float(E - 1), None, ALU.min))
            step(v.tensor_scalar(plan[:, 2, :], plan[:, 3, :], -1.0, float(E - 1), ALU.mult, ALU.add))
            step(v.tensor_copy(table[:, 0, :], plan[:, 2, :]))
            step(v.tensor_scalar(plan[:, 3, :], plan[:, 3, :], 16.0, 16.0, ALU.mult, ALU.add))
            v.tensor_copy(table[:, 2, :], plan[:, 3, :]).then_inc(plan_ready, 1)

            def expert_of(g):
                return dve.value_load(table[0:1, 0, bass.ds(g, 1)], min_val=0, max_val=E - 1)

            def lower(out, whole, upper, done):
                v.tensor_tensor(out, whole, upper.bitcast(F32), ALU.subtract).then_inc(done, 1)

            def fc_lower(g, par):
                e = expert_of(g)
                for a in range(DH):
                    dve.wait_ge(fc_hi_ready, g * 2 + a + 1)
                    lower(fc_lo[par][:, a, :], w_ffn[:, bass.ds(e, 1), a * DFF:(a + 1) * DFF].rearrange("p a f -> p (a f)"),
                          fc_hi[par][:, a, :], fc_lo_ready)

            def x_lower(g):
                dve.wait_ge(x_hi_ready, g + 1)
                lower(x_lo[:, :, :], psS[:, :].rearrange("p (h n) -> p h n", h=DH), x_hi[:, :, :], x_lo_ready)

            def hidden(g, c):
                dve.wait_ge(gelu_done, g * 4 + c + 1)
                v.tensor_copy(h_hi[:, 2 * c:2 * c + 2, :], h[:, c % 2]).then_inc(h_hi_ready, 1)
                dve.wait_ge(h_hi_ready, g * 4 + c + 1)
                lower(h_lo[:, 2 * c:2 * c + 2, :], h[:, c % 2], h_hi[:, 2 * c:2 * c + 2, :], h_ready)

            def slot_meta(g):
                at = E - 1 - expert_of(g) + ROW_W
                alone(xg_loaded, g * 16 + 16)
                v.tensor_copy(slot_w[:, bass.ds(g, 1), :].rearrange("p a s -> p s a"), xg[:, :, bass.ds(at, 1)]).then_inc(meta_read, 1)
                v.tensor_copy(slot_id[:, bass.ds(g, 1), :].rearrange("p a s -> p s a"),
                              xg[:, :, ROW_ID:ROW_ID + 1].bitcast(I32)).then_inc(meta_read, 1)

            def dve_group(g, par):
                hidden(g, 0)
                hidden(g, 1)
                if g_on(g + 1):
                    slot_meta(g + 1)
                hidden(g, 2)
                hidden(g, 3)
                if g_on(g + 1):
                    x_lower(g + 1)
                    fc_lower(g + 1, 1 - par)

            after_attention(dve)
            dve.sem_inc(dve_passed, 1)
            fc_lower(0, 0)
            x_lower(0)
            slot_meta(0)
            run_groups(dve, dve_group)

        @block.tensor
        def _(pe):
            mm = nc.tensor.matmul
            pe.wait_ge(ld_qkvo, 16 * 4)
            for w, m, bank in ((wq, wk, psG), (wv, wo_t, psV)):
                for a in range(DH):
                    for e in range(DH):
                        ins = mm(bank[:, a * D:(a + 1) * D], w[:, e, a * P:(a + 1) * P], m[:, e, :],
                                 start=(e == 0), stop=(e == DH - 1))
                ins.then_inc(qkvo_mm, 1)
            pe.wait_ge(ld_emb, 16 * 5)
            pe.wait_ge(sin_ready, 1)
            mm(psT1[:, 0:HT], temb_rw[:, :], emb[:, :], start=True, stop=True)
            mm(psT1[:, HT:2 * HT], temb_iw[:, :], emb[:, :], start=True, stop=True).then_inc(temb_mm, 1)
            pe.wait_ge(mix_built, 3 * NG)
            pe.wait_ge(temb_ready, 1)
            for og in range(NG):
                for g in range(NG):
                    ins = mm(psI[:, og * HT:(og + 1) * HT],
                             mix_abs[:, g, og * 4:(og + 1) * 4].rearrange("p o x c -> p (o x c)"), tabs[:, :],
                             start=(g == 0), stop=(g == NG - 1))
            ins.then_inc(norm_mm, 1)
            pe.wait_ge(ld_gn, 16)
            with pe.Fori(0, 4) as c:
                pe.wait_ge(gn_stats, c + 1)
                mm(psT2[:, 0:16], group[:, :], gmv[:, :, :], start=True, stop=True).then_inc(gn_mm, 1)
            pe.wait_ge(ld_conv, 16 * 4)
            pe.wait_ge(gn_done, NT)
            pe.wait_ge(qkvo_ready, 2)
            for g in range(NG):
                for j in range(4):
                    for hh in range(DH):
                        ins = mm(banks[g][32 * j:32 * j + 32, 0:B * HT], dft[:, hh, :],
                                 xc[:, hh, :].rearrange("p (n i) -> p i n", i=WI)[:, 4 * g + j, :],
                                 start=(hh == 0), stop=(hh == DH - 1))
                ins.then_inc(dft_mm, 1)
            pe.wait_ge(inv_ready, 1)
            for og in range(NG):
                for g in range(NG):
                    for n, (w, z) in enumerate(((mix_r, zr), (mix_i, zi))):
                        if og == 0:
                            pe.wait_ge(z_ready, 2 * g + n + 1)
                        ins = mm(banks[4 + og][:, 0:B * HT],
                                 w[:, g, og * 4:(og + 1) * 4].rearrange("p o x c -> p (o x c)"),
                                 z[:, g].rearrange("p b t -> p (b t)"), start=(g == 0 and n == 0),
                                 stop=(g == NG - 1 and n == 1))
                ins.then_inc(mix_mm, 1)

            pe.wait_ge(ld_attn, 16 * 4)

            def idft_of(b):
                pe.wait_ge(spec_copied, b + 1)
                if later(b):
                    pe.wait_ge(x1_ready, b)
                for s in range(2):
                    ins = mm(psI[:, s * D:(s + 1) * D], spec_b[:, s * P:(s + 1) * P], idft[:, :], start=True, stop=True)
                ins.then_inc(idft_mm, 1)

            def transposes(b, rows, bank, ready, done, bank_read):
                pe.wait_ge(ready, b * 2 + 2)
                if later(b):
                    pe.wait_ge(*bank_read(b))
                for hh in range(DH):
                    for s in range(2):
                        ins = nc.tensor.transpose(bank[:, hh * SEQ + s * P:hh * SEQ + (s + 1) * P],
                                                  rows[:, s, hh * P:(hh + 1) * P], ident[:, :])
                ins.then_inc(done, 1)

            def project(b):
                pe.wait_ge(xnt_ready, b + 1)
                if later(b):
                    pe.wait_ge(gt_ready, b)
                for a in range(DH):
                    for hh in range(DH):
                        ins = mm(psG[:, a * SEQ:(a + 1) * SEQ], qk_w[:, hh, a * P:(a + 1) * P], xn_t[:, hh, :],
                                 start=(hh == 0), stop=(hh == DH - 1))
                ins.then_inc(g_mm, 1)
                if later(b):
                    pe.wait_ge(v_ready, b)
                for s in range(2):
                    for hh in range(DH):
                        ins = mm(psV[:, s * D:(s + 1) * D], xn_t[:, hh, s * P:(s + 1) * P], vo_w[:, hh, :],
                                 start=(hh == 0), stop=(hh == DH - 1))
                ins.then_inc(v_mm, 1)

            def route(b):
                pe.wait_ge(xn2t_ready, b + 1)
                for s in range(2):
                    for hh in range(DH):
                        ins = mm(psT2[:, s * E:(s + 1) * E], xn2_t[:, hh, s * P:(s + 1) * P],
                                 router[:, hh, :], start=(hh == 0), stop=(hh == DH - 1))
                ins.then_inc(r_mm, 1)

            def count_before(b):
                pe.wait_ge(before_ready, b * 2 + 2)
                if b_in_scores(b):
                    pe.wait_ge(s_masked, (b + 3) * 2)
                for s in range(2):
                    mm(psS[:, s * E:(s + 1) * E], counting[:, 0, :], picked[:, s], start=True, stop=False)
                    ins = mm(psS[:, s * E:(s + 1) * E], counting[:, 1, :], before[:, s], start=False, stop=True)
                ins.then_inc(where_mm, 1)

            def b_in_scores(b):
                return not isinstance(b, int) or b + 3 <= B

            def scores(b):
                pe.wait_ge(gt_ready, b + 1)
                if later(b):
                    pe.wait_ge(s_masked, b * 2)
                if not isinstance(b, int) or b >= 3:
                    pe.wait_ge(where_read, b - 2)
                for s in range(2):
                    for hh in range(DH):
                        ins = mm(psS[:, s * P:(2 * s + 1) * P], g_t[:, hh, s * P:(s + 1) * P],
                                 xn_t[:, hh, 0:(s + 1) * P], start=(hh == 0), stop=(hh == DH - 1))
                ins.then_inc(s_mm, 1)

            def probs_t(b):
                pe.wait_ge(probs_ready, b * 2 + 2)
                if later(b):
                    pe.wait_ge(pt_ready, b)
                for n in range(3):
                    ins = nc.tensor.transpose(psP[:, n * P:(n + 1) * P], p_b[:, n * P:(n + 1) * P], ident[:, :])
                ins.then_inc(pt_mm, 1)

            def attend(b):
                pe.wait_ge(pt_ready, b + 1)
                pe.wait_ge(v_ready, b + 1)
                if later(b):
                    pe.wait_ge(x2_ready, b * 2)
                mm(psO[:, 0:D], p_t[:, 0:P], v_b[:, 0, :], start=True, stop=True)
                mm(psO[:, D:2 * D], p_t[:, P:2 * P], v_b[:, 0, :], start=True, stop=False)
                mm(psO[:, D:2 * D], p_t[:, 2 * P:3 * P], v_b[:, 1, :], start=False, stop=True).then_inc(pv_mm, 1)

            def pe_slot(k):
                if on(k):
                    transposes(k, xn, psT1, xn_ready, t1_mm, lambda b: (xnt_ready, b))
                    project(k)
                if on(k - 2):
                    transposes(k - 2, xn2, psT2, xn2_ready, t2_mm, lambda b: (gap_ready, b))
                if on(k - 1):
                    probs_t(k - 1)
                if on(k + 1):
                    idft_of(k + 1)
                if on(k - 1):
                    attend(k - 1)
                if on(k - 2):
                    route(k - 2)
                if on(k - 3):
                    count_before(k - 3)
                if on(k):
                    scores(k)

            idft_of(0)
            for k in FIRST_SLOTS:
                pe_slot(k)
            with pe.Fori(*LOOP_SLOTS) as k:
                pe_slot(k)
            for k in LAST_SLOTS:
                pe_slot(k)
            pe.wait_ge(plan_step, 1)
            pe.wait_ge(where_read, B)
            mm(psS[:, 0:E], counting[:, 1, :], before[:, 0], start=True, stop=True).then_inc(counts_mm, 1)

            def three(w_hi, w_lo, m_hi, m_lo):
                return (w_hi, m_hi), (w_hi, m_lo), (w_lo, m_hi)

            def x_transposes(g):
                pe.wait_ge(xg_loaded, g * 16 + 16)
                if later(g):
                    pe.wait_ge(x_lo_ready, g)
                for hh in range(DH):
                    for s in range(2):
                        ins = nc.tensor.transpose(psS[:, hh * GS + s * P:hh * GS + (s + 1) * P],
                                                  xg[:, s, hh * P:(hh + 1) * P], ident[:, :])
                ins.then_inc(xg_t_mm, 1)

            def up(g, par):
                pe.wait_ge(x_lo_ready, g + 1)
                pe.wait_ge(fc_lo_ready, g * 2 + 2)
                for f in range(FC):
                    c = f // 2
                    if f % 2 == 0 and later(g):
                        pe.wait_ge(gelu_done, g * 4 + c - 3)
                    n = 0
                    for w, m in three(fc_hi[par], fc_lo[par], x_hi, x_lo):
                        for hh in range(DH):
                            ins = mm(banks[c][:, (f % 2) * GS:(f % 2 + 1) * GS], w[:, hh, f * P:(f + 1) * P], m[:, hh, :],
                                     start=(n == 0), stop=(n == 5))
                            n += 1
                    if f % 2:
                        ins.then_inc(up_mm, 1)

            def down(g):
                if later(g):
                    pe.wait_ge(y_ready, g * 2)
                for f in range(FC):
                    if f % 4 == 0:
                        pe.wait_ge(pj_lo_ready, g * 2 + f // 4 + 1)
                    if f % 2 == 0:
                        pe.wait_ge(h_ready, g * 4 + f // 2 + 1)
                    for s, bank in enumerate((psP, psO)):
                        for n, (w, m) in enumerate(three(h_hi, h_lo, pj_hi, pj_lo)):
                            ins = mm(bank[:, 0:D], w[:, f, s * P:(s + 1) * P], m[:, f, :],
                                     start=(f == 0 and n == 0), stop=(f == FC - 1 and n == 2))
                    if f % 4 == 3:
                        ins.then_inc(down_mm, 1)

            def pe_group(g, par):
                up(g, par)
                if g_on(g + 1):
                    x_transposes(g + 1)
                down(g)

            x_transposes(0)
            run_groups(pe, pe_group)


def laid_out(i):
    f = {n: np.asarray(a) for n, a in i.items()}
    flat = f["x"].reshape(TOK, D)
    w = f["L0_conv_weights1"]
    swapped = w[..., ::-1]
    mixr = np.stack([w, swapped], axis=3)
    mixi = np.stack([swapped, w], axis=3)

    def rows(a):
        return np.ascontiguousarray(a.transpose(0, 2, 3, 1, 4).reshape(NG, P, WI, 2).transpose(1, 0, 2, 3))

    ke = f["L0_conv_ke_weights"]
    temb_w = []
    for c in range(2):
        full = np.zeros((HEADS, MIDCH // HEADS, HEADS, MODES, 2), ke.dtype)
        for hd in range(HEADS):
            full[hd, :, hd] = ke[hd, :, c::2, None]
        temb_w.append(full.reshape(MIDCH, P))
    kb = f["L0_conv_ke_bias"].reshape(MODES, 2)
    bias = np.broadcast_to(kb[None, :, None, :], (4, MODES, 2, 2)).reshape(P, 2)
    w_fc = f["L1_ffn_w_fc"].reshape(E, DH, P, DFF).transpose(0, 2, 1, 3).reshape(E, P, DH * DFF)
    w_proj = f["L1_ffn_w_proj"].reshape(E, FC, P, D).transpose(0, 2, 1, 3).reshape(E, P, FC * D)
    w_ffn = np.concatenate([w_fc, w_proj], axis=2)
    return {
        "x_tok": flat, "x_ch": flat.T, "t": f["L0_conv_t"], "mixr_w": rows(mixr), "mixi_w": rows(mixi),
        "temb_rw": temb_w[0], "temb_iw": temb_w[1], "bias": bias, "wq": f["L1_attn_W_q"], "wk": f["L1_attn_W_k"],
        "wv": f["L1_attn_W_v"], "wo_t": f["L1_attn_W_o"].T, "router": f["L1_ffn_router_w"],
        "w_ffn": w_ffn,
    }


def kernel(**inputs):
    import concourse.bacc as bacc
    from concourse.bass_utils import run_bass_kernel_spmd

    nc = bacc.Bacc("TRN2", target_bir_lowering=False, num_devices=1)
    arrays, args = {}, []
    for name, a in {**laid_out(inputs), **constants()}.items():
        a = np.ascontiguousarray(a)
        arrays["in_" + name] = a
        args.append(nc.dram_tensor("in_" + name, a.shape, mybir.dt.from_np(a.dtype), kind="ExternalInput").ap())
    args.append(nc.dram_tensor("out", (TOK + GS, D), F32, kind="ExternalOutput").ap())
    args.append(nc.dram_tensor("slots", (IDLE_ROW + GS, ROW), F32, kind="Internal").ap())
    hybrid_block(nc, *args)
    r = run_bass_kernel_spmd(nc, [arrays], core_ids=[0])
    return r.results[0]["out"][:TOK].reshape(B, HT, WI, D)
```

```python
from contextlib import ExitStack

import numpy as np
import concourse.bass as bass
from concourse import mybir

F32 = mybir.dt.float32
BF16 = mybir.dt.bfloat16
F32R = mybir.dt.float32r
I32 = mybir.dt.int32
ALU = mybir.AluOpType
ACT = mybir.ActivationFunctionType
AX_X = mybir.AxisListType.X

P = 128
B, HT, WI, D = 16, 16, 16, 256
TOK = B * HT * WI
SEQ = HT * WI
NT = TOK // P
DH = D // P
MODES = 16
MC = 2 * MODES
NG = WI * MC // P
HEADS, MIDCH = 4, 32
CHUNKS = 4
CB = B // CHUNKS
CT = CB * DH
GN_EPS, LN_EPS = 1e-5, 1e-5
E, DFF = 8, 1024
FC = DFF // P
PICKS = 2

PAIRS = B // 2
EARLY_PAIRS = PAIRS - 2
PT = NT // PAIRS
WHERE = 64

GS = 256
GROUPS = (TOK * PICKS - E) // GS + E
ROW_W, ROW_ID = D, D + E
ROW = D + E + 1
REGION = TOK + GS
LATE = 3
LATE_BEHIND = 3, 5, 7
assert LATE_BEHIND[-1] < TOK // GS
IDLE_ROW = E * REGION

MASKED = -2.0 ** 100
MAGIC = 1.5 * 2.0 ** 23
TWO_PI = 2.0 * np.pi
PI_LOW = 3.1415925


def two_pi_parts():
    parts, rest = [], TWO_PI
    for _ in range(3):
        step = 2.0 ** (np.floor(np.log2(rest)) - 8)
        parts.append(float(np.floor(rest / step) * step))
        rest -= parts[-1]
    return parts + [float(np.float32(rest))]


TIME_PARTS = (P, P, 3, HT)
CONV_PARTS = (NG * WI * 2, NG * WI * 2, 3 * MC, DH * MC, P, 2)
ATTN_PARTS = (P, P, 2 * P, 2 * PT * E, DH * E)


def split(a, parts):
    ends = np.cumsum(parts)
    return [a[:, int(end - n):int(end)] for end, n in zip(ends, parts)]


def constants():
    l = np.arange(D)
    x = np.arange(MODES)
    angle = 2 * np.pi * np.outer(l, x) / D
    dft = np.stack([np.cos(angle), -np.sin(angle)], axis=-1).reshape(D, MC)
    weight = np.where(x == 0, 1.0, 2.0)[:, None] / D
    idft = np.stack([np.cos(angle.T) * weight, -np.sin(angle.T) * weight], axis=1).reshape(MC, D)
    same_mode = np.repeat(np.repeat(np.eye(MODES), 2, 0), 2, 1)
    c, c2 = np.arange(MC)[:, None] % 2, np.arange(MC)[None, :] % 2
    sign_r = np.where((c == 1) & (c2 == 0), -1.0, 1.0)
    sign_i = np.where((c == 0) & (c2 == 1), 1.0, -1.0)
    masks = np.stack([same_mode * sign_r, same_mode * sign_i, same_mode * (c == 0)], axis=1)
    masks = np.tile(masks, (4, 1, 1))
    q, k = np.arange(P)[:, None], np.arange(P)[None, :]
    causal = np.where(k <= q, 0.0, MASKED)
    half = MIDCH // 2
    steps = -np.float32(np.log(10000.0)) * np.arange(half, dtype=np.float32) / np.float32(half)
    freqs = np.exp(steps.astype(np.float64)).astype(np.float32)
    angles = np.stack([np.tile(freqs, 2), np.repeat([1.0, 0.0], half), np.repeat([0.0, 1.0], half)], axis=1)
    f = np.float32
    fill = np.zeros((P, 2, ROW), np.float32)
    fill.view(np.int32)[:, :, ROW_ID] = TOK + np.arange(2)[None, :] * P + np.arange(P)[:, None]
    ids = (np.arange(NT)[None, :] * P + np.arange(P)[:, None]).astype(np.int32)
    experts = np.stack([np.tile(E - np.arange(E), (P, PT, 1)), np.tile(REGION * np.arange(E), (P, PT, 1))], axis=1)
    counting = np.stack([np.triu(np.ones((P, P)), 1), np.ones((P, P))], axis=1)
    numbers = np.broadcast_to(np.arange(GROUPS)[None, :, None], (P, GROUPS, E))
    return {
        "dft": dft.astype(f), "masks": masks.astype(f), "group": np.kron(np.eye(P // 8), np.full((8, 8), 1 / 8)).astype(f),
        "angles": angles.astype(f), "causal": causal.astype(f), "counting": counting.astype(f), "experts": experts.astype(f),
        "ident": np.eye(P, dtype=f), "idft": idft.astype(f), "fill": fill, "ids": ids, "numbers": numbers.astype(f),
    }


def hybrid_block(nc, x_tok_d, x_ch_d, time_in_d, conv_in_d, w_in_d, attn_in_d, w_ffn_d, c_ident_d, c_idft_d, c_fill_d,
                 c_ids_d, c_numbers_d, out_d, slots_d):
    with ExitStack() as ctx:
        start = -(-nc.sbuf_base // 32) * 32
        ctx.enter_context(nc.sbuf_tensor("arena", [P, nc.sbuf_usable_end - start - 64], mybir.dt.uint8))
        filled = {}

        def place(area, name, shape, dt=F32):
            at = filled.setdefault(area, AREAS[area][0])
            size = -(-int(np.prod(shape[1:])) * 4 // 32) * 32
            assert at + size <= AREAS[area][1], (area, name)
            filled[area] = at + size
            return nc.alloc_sbuf_tensor_at(name, shape, dt, offset=start + at)

        EXPERT = (DH * DFF + FC * D) * 4
        SENT_BYTES = 6912
        end = (nc.sbuf_usable_end - start - 64) // 32 * 32
        weights_at = end - E * EXPERT
        AREAS = {
            "always": (0, 2560),
            "ffn": (2560, weights_at),
            "weights": (weights_at, end),
            "attention": (2560, weights_at + LATE * EXPERT - SENT_BYTES),
            "sent": (weights_at + LATE * EXPERT - SENT_BYTES, weights_at + LATE * EXPERT),
            "conv": (weights_at + LATE * EXPERT, end),
        }

        def at(name, shape, dt=F32):
            return place("attention", name, shape, dt)

        def cv(name, shape, dt=F32):
            return place("conv", name, shape, dt)

        def ff(name, shape, dt=F32):
            return place("ffn", name, shape, dt)

        def ps(name):
            return ctx.enter_context(nc.psum_tensor(name, [P, 512], F32))

        def sem(name):
            return ctx.enter_context(nc.semaphore(name))

        ident = place("always", "ident", [P, P])
        slot_w = place("always", "slot_w", [P, GROUPS, 2])
        slot_id = place("always", "slot_id", [P, GROUPS, 2], I32)
        table = place("always", "table", [P, 4, GROUPS], I32)
        late_need = place("always", "late_need", [P, LATE - 1], I32)
        first_need = place("always", "first_need", [P, 1], I32)
        add_id = place("always", "add_id", [P, 2], I32)

        xc = cv("xc", [P, DH, TOK])
        time_in = cv("time_in", [MIDCH, sum(TIME_PARTS)])
        temb_rw, temb_iw, angles, t_row = split(time_in[:, :], TIME_PARTS)
        conv_in = cv("conv_in", [P, sum(CONV_PARTS)])
        mixr_w, mixi_w, masks, dft, group, bias = split(conv_in[:, :], CONV_PARTS)
        mixr_w, mixi_w = (a.rearrange("p (g o c) -> p g o c", g=NG, o=WI) for a in (mixr_w, mixi_w))
        masks = masks.rearrange("p (n m) -> p n m", n=3)
        dft = dft.rearrange("p (h m) -> p h m", h=DH)
        idft = cv("idft", [MC, D])
        w_in = cv("w_in", [P, 4, DH, D])
        wq, wk, wv, wo_t = (w_in[:, n] for n in range(4))
        mix_r = cv("mix_r", [P, NG, WI, MODES, 2])
        mix_i = cv("mix_i", [P, NG, WI, MODES, 2])
        mix_abs = cv("mix_abs", [P, WI, MODES, 2])
        sq = cv("sq", [P, NG * WI, 2])
        wsq = cv("wsq", [P, NG * WI])
        wabs = cv("wabs", [P, NG * WI])
        wabs_sum = cv("wabs_sum", [P, WI])
        ang = cv("ang", [MIDCH, 4, HT])
        emb = cv("emb", [MIDCH, HT])
        temb = cv("temb", [P, 2, HT])
        tsq = cv("tsq", [P, 2, HT])
        tpow = cv("tpow", [P, HT])
        tabs = cv("tabs", [P, HT])
        inv = cv("inv", [P, NG * HT])
        gst = cv("gst", [P, CHUNKS, CT, 6])
        gmv = cv("gmv", [P, CHUNKS, CT, 2])
        ggm = cv("ggm", [P, CHUNKS, CT, 2])
        gsq = cv("gsq", [P, CHUNKS, CT])
        gvar = cv("gvar", [P, CHUNKS, CT])
        gsd = cv("gsd", [P, CHUNKS, CT])
        grs = cv("grs", [P, CHUNKS, CT])
        gnb = cv("gnb", [P, CHUNKS, CT])
        zr = at("zr", [P, NG, B, HT])
        zi = at("zi", [P, NG, B, HT])

        x = at("x", [P, NT, D])
        power = at("power", [P, 4])
        attn_in = at("attn_in", [P, sum(ATTN_PARTS)])
        ident_in, causal, counting, experts, router = split(attn_in[:, :], ATTN_PARTS)
        counting = counting.rearrange("p (n q) -> p n q", n=2)
        experts = experts.rearrange("p (n t e) -> p n t e", n=2, t=PT)
        router = router.rearrange("p (h e) -> p h e", h=DH)
        causal_16 = at("causal_16", [P, P], BF16)
        ident_16 = at("ident_16", [P, P], BF16)
        spec_parts = at("spec_parts", [3 * MC, SEQ], F32R)
        idft_parts = at("idft_parts", [3 * MC, D], F32R)
        ids = place("sent", "ids", [P, NT], I32)
        fill = place("sent", "fill", [P, 2, ROW])
        spec = at("spec", [MC, TOK])
        qk_w = at("qk_w", [P, DH, D])
        vo_w = at("vo_w", [P, DH, D])
        st = at("st", [P, 4, 6])
        mv = at("mv", [P, 4, 2])
        rs = at("rs", [P, 4])
        xn = at("xn", [P, 2, D])
        xn2 = at("xn2", [P, 2, D])
        xn2_kept = at("xn2_kept", [P, NT, D])
        row = [place("sent", f"row{n}", [P, 2, ROW]) for n in range(2)]
        xn_t = at("xn_t", [P, DH, SEQ])
        xn2_t = at("xn2_t", [P, DH, SEQ])
        g_t = at("g_t", [P, DH, SEQ])
        v_b = at("v_b", [P, 2, D])
        p_b = at("p_b", [P, 3 * P])
        p_t = at("p_t", [P, 3 * P])
        nmax = at("nmax", [P, 2])
        rsum = at("rsum", [P, 2])
        rinv = at("rinv", [P, 2])
        logits = at("logits", [P, PT, E])
        hot = at("hot", [P, PICKS, PT, E])
        cand = at("cand", [P, PT, E])
        rest = at("rest", [P, PT, E])
        best = at("best", [P, PICKS, PT])
        key = at("key", [P, PT])
        gap = at("gap", [P, PT])
        ratio = at("ratio", [P, PT])
        pick_w = at("pick_w", [P, PICKS, PT])
        part = at("part", [P, PICKS, PT, E])
        weights = place("sent", "weights", [P, PT, E])
        picked = at("picked", [P, PT, E])
        before = at("before", [P, PT, E])
        where = at("where", [P, PT, E])
        slot_f = at("slot_f", [P, PICKS, PT])
        slot, *slot_ending = (place("always", n, [P, PICKS, PT], I32) for n in ("slot", "slot_ending0", "slot_ending1"))
        need = at("need", [P, 1])
        behind_f = at("behind_f", [P, LATE - 1])
        counts = at("counts", [P, 4, E])
        tail_f = at("tail_f", [P, E])
        tail = place("always", "tail", [P, E], I32)
        numbers = at("numbers", [P, GROUPS, E])
        past = at("past", [P, GROUPS, E])
        past_end = at("past_end", [P, GROUPS, E])
        plan = at("plan", [P, 4, GROUPS])

        w_ffn = place("weights", "w_ffn", [P, E, DH * DFF + FC * D])
        xg = ff("xg", [P, 2, ROW])
        fc_hi = [ff(f"fc_hi{n}", [P, DH, DFF], F32R) for n in range(2)]
        fc_lo = [ff(f"fc_lo{n}", [P, DH, DFF], F32R) for n in range(2)]
        pj_hi, pj_lo = (ff(n, [P, FC, D], F32R) for n in ("pj_hi", "pj_lo"))
        h_hi, h_lo = (ff(n, [P, FC, GS], F32R) for n in ("h_hi", "h_lo"))
        h = ff("h", [P, 2, 2, GS])
        x_hi, x_lo = (ff(n, [P, DH, GS], F32R) for n in ("x_hi", "x_lo"))
        y = ff("y", [P, 2, D])

        psT1, psT2, psG, psV, psS, psP, psO, psI = banks = [ps(n) for n in (
            "psT1", "psT2", "psG", "psV", "psS", "psP", "psO", "psI")]
        ld_emb, ld_qkvo, ld_conv, ld_attn, ld_ident, ld_idft = (
            sem(n) for n in ("ld_emb", "ld_qkvo", "ld_conv", "ld_attn", "ld_ident", "ld_idft"))
        ld_x = [sem("ld_x_first"), sem("ld_x_rest")]
        ld_xc = [sem(f"ld_xc{c}") for c in range(CHUNKS)]
        emb_step, emb_ready, sin_ready, temb_mm, temb_step, temb_ready = (
            sem(n) for n in ("emb_step", "emb_ready", "sin_ready", "temb_mm", "temb_step", "temb_ready"))
        mix_built, wabs_step, wabs_ready, norm_mm, inv_step, inv_ready = (
            sem(n) for n in ("mix_built", "wabs_step", "wabs_ready", "norm_mm", "inv_step", "inv_ready"))
        qkvo_mm, qkvo_ready = sem("qkvo_mm"), sem("qkvo_ready")
        gn_step, gn_stats, gn_mm, gn_var, gn_sd, gn_rs, gn_done, gn_done_dve = (
            sem(n) for n in ("gn_step", "gn_stats", "gn_mm", "gn_var", "gn_sd", "gn_rs", "gn_done", "gn_done_dve"))
        dft_mm, z_ready, mix_mm, spec_ready = (sem(n) for n in ("dft_mm", "z_ready", "mix_mm", "spec_ready"))
        idft_step, idft_ready = sem("idft_step"), sem("idft_ready")
        spec_upper, spec_upper_act, idft_mm, x1_ready, xn_ready = (
            sem(n) for n in ("spec_upper", "spec_upper_act", "idft_mm", "x1_ready", "xn_ready"))
        stats_ready, mv_ready, var_ready, rs_ready = (
            [sem(f"{n}{norm}") for norm in (1, 2)] for n in ("stats_ready", "mv_ready", "var_ready", "rs_ready"))
        t1_mm, xnt_ready, g_mm, gt_ready, v_mm, v_ready, s_mm = (
            sem(n) for n in ("t1_mm", "xnt_ready", "g_mm", "gt_ready", "v_mm", "v_ready", "s_mm"))
        mask_ready, nmax_ready, probs_ready, pt_mm, pt_ready, pv_mm, rinv_ready = (
            sem(n) for n in ("mask_ready", "nmax_ready", "probs_ready", "pt_mm", "pt_ready", "pv_mm", "rinv_ready"))
        x2_ready, xn2_ready, t2_mm, xn2t_ready, r_mm, logits_ready = (
            sem(n) for n in ("x2_ready", "xn2_ready", "t2_mm", "xn2t_ready", "r_mm", "logits_ready"))
        power_ready = sem("power_ready")
        ld_route, ld_numbers, row_ready, pick_step, ones_ready = (
            sem(n) for n in ("ld_route", "ld_numbers", "row_ready", "pick_step", "ones_ready"))
        pool_passed, dve_passed, sp_passed, act_passed = (
            sem(n) for n in ("pool_passed", "dve_passed", "sp_passed", "act_passed"))
        kept, top_step, gap_ready, ratio_ready, weights_ready, before_ready = (
            sem(n) for n in ("kept", "top_step", "gap_ready", "ratio_ready", "weights_ready", "before_ready"))
        where_mm, where_read, slot_step, slot_ready, row_filled, x2_stored = (
            sem(n) for n in ("where_mm", "where_read", "slot_step", "slot_ready", "row_filled", "x2_stored"))
        scattered = [sem("scattered_even"), sem("scattered_odd")]
        spec_lower = sem("spec_lower")
        wabs_summed, exp_loaded = sem("wabs_summed"), sem("exp_loaded")
        need_step, slots_complete, late_ready = sem("need_step"), sem("slots_complete"), sem("late_ready")
        rows_ready = sem("rows_ready")
        counts_mm, plan_step, plan_ready, filled_up, idle_stored = (
            sem(n) for n in ("counts_mm", "plan_step", "plan_ready", "filled_up", "idle_stored"))
        ld_w = sem("ld_w")
        xg_loaded, xg_t_mm, x_hi_ready, x_lo_ready, meta_read, up_mm, gelu_done, h_hi_ready, h_ready = (
            sem(n) for n in ("xg_loaded", "xg_t_mm", "x_hi_ready", "x_lo_ready", "meta_read", "up_mm", "gelu_done", "h_hi_ready", "h_ready"))
        fc_hi_ready, fc_lo_ready, pj_hi_ready, pj_lo_ready, down_mm, y_ready, id_ready, y_added = (
            sem(n) for n in ("fc_hi_ready", "fc_lo_ready", "pj_hi_ready", "pj_lo_ready", "down_mm", "y_ready", "id_ready", "y_added"))

        def gn_tile(c, n):
            at = (c * CB + n // DH) * SEQ
            return xc[:, n % DH, at:at + SEQ]

        def on(b):
            return not isinstance(b, int) or 0 <= b < B

        def later(b):
            return not isinstance(b, int) or b > 0

        def weights_in(eng, e):
            if e:
                eng.wait_ge(ld_w, 16 * e)
            eng.dma_start(w_ffn[:, (e + LATE) % E, :], w_ffn_d[e]).then_inc(ld_w, 16)

        def slots_there(eng):
            for half in range(2):
                eng.wait_ge(scattered[half], SENT * PAIRS)
            eng.wait_ge(filled_up, 16 * E)

        def load_group(eng, g):
            at_row = eng.value_load(table[0:1, 1, bass.ds(g, 1)], min_val=0, max_val=IDLE_ROW)
            eng.dma_start(xg[:, :, :], slots_d[bass.ds(at_row, GS)].rearrange("(s p) r -> p s r", p=P)).then_inc(xg_loaded, 16)

        def after_attention(eng):
            eng.wait_ge(x2_stored, 16 * (B + 1))
            eng.wait_ge(row_filled, B)
            eng.wait_ge(counts_mm, 1)
            eng.wait_ge(plan_ready, 2)
            eng.wait_ge(late_ready, 1)

        SENT = 16 * 2 * PICKS

        NORM_TILES = slice(0, 2), slice(2, 4)

        def ending(j):
            return isinstance(j, int) and j >= PAIRS - 2

        def slots_of(j):
            return slot_ending[j - (PAIRS - 2)] if ending(j) else slot

        def counts_bank(j):
            return psG if ending(j) else psT2

        def g_on(g):
            return not isinstance(g, int) or 0 <= g < GROUPS

        def run_groups(eng, body):
            body(0, 0)
            pairs = (GROUPS - 2) // 2
            with eng.Fori(0, pairs) as i:
                body(i * 2 + 1, 1)
                body(i * 2 + 2, 0)
            for g in range(1 + 2 * pairs, GROUPS):
                body(g, g % 2)

        def on_pair(j):
            return not isinstance(j, int) or 0 <= j < PAIRS

        def run_attention(eng, body):
            for k in range(-1, 5):
                body(k, k % 2, (k - 4) // 2)
            with eng.Fori(0, (B - 8) // 2) as i:
                body(i * 2 + 5, 1, i)
                body(i * 2 + 6, 0, i + 1)
            for k in range(B - 3, B + 5):
                body(k, k % 2, (k - 4) // 2)

        block = ctx.enter_context(nc.Block())

        @block.sync
        def _(sp):
            sp.dma_start(time_in[:, :], time_in_d).then_inc(ld_emb, 16)
            sp.dma_start(conv_in[:, :], conv_in_d).then_inc(ld_conv, 16)
            for c in range(CHUNKS):
                n = TOK // CHUNKS
                sp.dma_start(xc[:, :, c * n:(c + 1) * n],
                             x_ch_d.rearrange("(h p) n -> p h n", p=P)[:, :, c * n:(c + 1) * n]).then_inc(ld_xc[c], 16)
            sp.dma_start(w_in[:, :, :, :], w_in_d).then_inc(ld_qkvo, 16)
            sp.dma_start(attn_in[:, :], attn_in_d).then_inc(ld_attn, 16)
            sp.dma_start(ident[:, :], c_ident_d).then_inc(ld_ident, 16)
            sp.dma_start(idft[:, :], c_idft_d).then_inc(ld_idft, 16)
            for n, at in enumerate((slice(0, NT // 4), slice(NT // 4, NT))):
                sp.dma_start(x[:, at, :], x_tok_d.rearrange("(n p) d -> p n d", p=P)[:, at, :]).then_inc(ld_x[n], 16)
            for dst, src in ((ids[:, :], c_ids_d), (fill[:, :, :], c_fill_d)):
                sp.dma_start(dst, src).then_inc(ld_route, 16)
            sp.dma_start(numbers[:, :, :], c_numbers_d).then_inc(ld_numbers, 16)
            sp.wait_ge(ld_route, 16 * 2)
            sp.dma_start(slots_d[IDLE_ROW:IDLE_ROW + GS].rearrange("(s p) r -> p s r", p=P), fill[:, :, :]).then_inc(idle_stored, 16)
            sp.dma_start(out_d[TOK:TOK + GS].rearrange("(s p) d -> p s d", p=P), fill[:, :, 0:D]).then_inc(x2_stored, 16)

            sp.wait_ge(mix_mm, NG)
            sp.wait_ge(qkvo_mm, 2)
            sp.wait_ge(exp_loaded, 1)
            sp.wait_ge(spec_ready, WI)
            for e in range(E - LATE):
                weights_in(sp, e)
            with sp.Fori(0, B) as b:
                sp.wait_ge(x2_ready, b * 2 + 2)
                sp.dma_start(out_d[bass.ds(b * SEQ, SEQ)].rearrange("(s p) d -> p s d", p=P),
                             x[:, bass.ds(b * 2, 2), :]).then_inc(x2_stored, 16)
            sp.wait_ge(plan_ready, 2)
            for e in range(E):
                at_row = sp.value_load(tail[0:1, e:e + 1], min_val=e * REGION, max_val=e * REGION + TOK)
                sp.dma_start(slots_d[bass.ds(at_row, GS)].rearrange("(s p) r -> p s r", p=P),
                             fill[:, :, :]).then_inc(filled_up, 16)
            after_attention(sp)
            slots_there(sp)
            sp.wait_ge(idle_stored, 16)
            sp.wait_ge(meta_read, 2)
            sp.wait_ge(xg_t_mm, 1)
            load_group(sp, 1)
            sp.wait_ge(late_ready, 1)
            for n in range(LATE):
                if n < LATE - 1:
                    behind = sp.value_load(late_need[0:1, n:n + 1], min_val=16, max_val=16 * LATE_BEHIND[n])
                    sp.wait_ge(xg_loaded, behind)
                    sp.sem_inc(sp_passed, 1)
                else:
                    sp.wait_ge(xg_loaded, 16 * LATE_BEHIND[n])
                weights_in(sp, E - LATE + n)
            sp.wait_ge(y_added, 32 * GROUPS)

        @block.gpsimd
        def _(pool):
            nc.gpsimd.memset(power[:, :], -0.5).then_inc(power_ready, 1)
            pool.wait_ge(power_ready, 1)
            pool.sem_inc(slots_complete, 1)
            pool.wait_ge(ld_conv, 16)
            for src, dst, m in ((mixr_w, mix_r, 0), (mixi_w, mix_i, 1)):
                for g in range(NG):
                    nc.gpsimd.tensor_tensor(
                        dst[:, g], src[:, g].unsqueeze(2).broadcast_to([P, WI, MODES, 2]),
                        masks[:, m].rearrange("p (a x c) -> p a x c", a=1, c=2).broadcast_to([P, WI, MODES, 2]),
                        ALU.mult).then_inc(mix_built, 1)
            pool.wait_ge(wabs_summed, 1)
            nc.gpsimd.tensor_tensor(
                mix_abs[:, :], wabs_sum[:, :].rearrange("p (o x c) -> p o x c", x=1, c=1).broadcast_to([P, WI, MODES, 2]),
                masks[:, 2].rearrange("p (a x c) -> p a x c", a=1, c=2).broadcast_to([P, WI, MODES, 2]),
                ALU.mult).then_inc(mix_built, 1)

            pool.wait_ge(ld_idft, 16)
            nc.gpsimd.tensor_copy(idft_parts[0:MC, :], idft[:, :]).then_inc(idft_step, 1)
            pool.wait_ge(idft_step, 1)
            pool.wait_ge(mix_built, 2 * NG + 1)
            nc.gpsimd.tensor_copy(idft_parts[2 * MC:, :], idft[:, :]).then_inc(idft_ready, 1)
            pool.wait_ge(idft_ready, 1)
            nc.gpsimd.tensor_tensor(idft_parts[MC:2 * MC, :], idft[:, :], idft_parts[0:MC, :].bitcast(F32),
                                    ALU.subtract).then_inc(idft_ready, 1)
            pool.wait_ge(idft_ready, 2)

            def gate():
                pool.sem_inc(pool_passed, 1)

            def rsqrt(b, norm):
                t = NORM_TILES[norm]
                pool.wait_ge(var_ready[norm], b + 1)
                nc.gpsimd.tensor_tensor(rs[:, t], rs[:, t], power[:, t], ALU.pow).then_inc(rs_ready[norm], 1)

            def split_spec(b):
                this = spec[:, bass.ds(b * SEQ, SEQ)]
                pool.wait_ge(idft_mm, b)
                gate()
                nc.gpsimd.tensor_copy(spec_parts[0:MC, :], this).then_inc(spec_upper, 1)
                pool.wait_ge(spec_upper, b + 1)
                gate()
                nc.gpsimd.tensor_tensor(spec_parts[2 * MC:, :], this, spec_parts[0:MC, :].bitcast(F32),
                                        ALU.subtract).then_inc(spec_lower, 1)
                pool.wait_ge(spec_lower, b + 1)
                gate()

            def scatter(b, half, j):
                pool.wait_ge(row_filled, b + 1)
                pool.wait_ge(weights_ready, j + 1)
                gate()
                tiles = slice(2 * half, 2 * half + 2)
                to = slots_of(j)
                nc.gpsimd.tensor_copy(row[half][:, :, ROW_W:ROW_W + E], weights[:, tiles, :]).then_inc(row_ready, 1)
                nc.gpsimd.tensor_copy(row[half][:, :, ROW_ID].bitcast(I32), ids[:, bass.ds(b * 2, 2)]).then_inc(row_ready, 1)
                pool.wait_ge(row_ready, b * 2 + 2)
                pool.wait_ge(slot_ready, j + 1)
                gate()
                for s in range(2):
                    t = 2 * half + s
                    for n in range(PICKS):
                        nc.gpsimd.indirect_dma_start(
                            slots_d, bass.IndirectOffsetOnAxis(ap=to[:, n, t:t + 1], axis=0), row[half][:, s, :],
                            None).then_inc(scattered[half], 16)

            def pool_slot(k, odd, j):
                first = isinstance(k, int) and k == -1
                if first:
                    split_spec(k + 2)
                if on(k + 1):
                    rsqrt(k + 1, 0)
                if on(k + 2) and not first:
                    split_spec(k + 2)
                if on(k - 1):
                    rsqrt(k - 1, 1)
                if on(k - 5):
                    scatter(k - 5, 0 if odd else 1, j if odd else j - 1)

            pool.wait_ge(ld_route, 16 * 2)
            run_attention(pool, pool_slot)

            def add(g):
                if later(g):
                    pool.wait_ge(y_added, g * 32)
                pool.wait_ge(meta_read, g * 2 + 2)
                gate()
                nc.gpsimd.tensor_copy(add_id[:, :], slot_id[:, bass.ds(g, 1), :]).then_inc(id_ready, 1)
                pool.wait_ge(y_ready, g * 2 + 2)
                pool.wait_ge(id_ready, g + 1)
                gate()
                for s in range(2):
                    nc.gpsimd.indirect_dma_start(
                        out_d, bass.IndirectOffsetOnAxis(ap=add_id[:, s:s + 1], axis=0), y[:, s, :], None,
                        compute_op=ALU.add).then_inc(y_added, 16)

            def proj_lower(g):
                e = pool.value_load(table[0:1, 0, bass.ds(g, 1)], min_val=0, max_val=E - 1)
                for a in range(2):
                    pool.wait_ge(pj_hi_ready, g * 2 + a + 1)
                    nc.gpsimd.tensor_tensor(
                        pj_lo[:, 4 * a:4 * a + 4, :],
                        w_ffn[:, bass.ds(e, 1), (2 + a) * DFF:(3 + a) * DFF].rearrange("p a (c d) -> p (a c) d", d=D),
                        pj_hi[:, 4 * a:4 * a + 4, :].bitcast(F32), ALU.subtract).then_inc(pj_lo_ready, 1)

            after_attention(pool)
            slots_there(pool)
            pool.sem_inc(slots_complete, 1)
            proj_lower(0)
            proj_lower(1)
            add(0)
            with pool.Fori(2, GROUPS) as g:
                proj_lower(g)
                add(g - 1)
            add(GROUPS - 1)

        @block.scalar
        def _(act):
            act.wait_ge(emb_ready, 1)
            nc.scalar.activation(emb[:, :], ang[:, 0, :], ACT.Sin).then_inc(sin_ready, 1)
            act.wait_ge(wabs_step, 2)
            nc.scalar.activation(wabs[:, :], wsq[:, :], ACT.Sqrt).then_inc(wabs_ready, 1)
            act.wait_ge(temb_step, 4)
            nc.scalar.activation(tabs[:, :], tpow[:, :], ACT.Sqrt).then_inc(temb_ready, 1)
            for c in range(CHUNKS):
                act.wait_ge(gn_var, c + 1)
                nc.scalar.activation(gsd[:, c, :], gvar[:, c, :], ACT.Sqrt).then_inc(gn_sd, 1)
                act.wait_ge(gn_rs, c + 1)
                for n in range(CT if c < CHUNKS - 1 else CT // 2):
                    tile = gn_tile(c, n)
                    nc.scalar.activation(tile, tile, ACT.Identity, scale=grs[:, c, n:n + 1],
                                         bias=gnb[:, c, n:n + 1]).then_inc(gn_done, 1)
            act.wait_ge(temb_ready, 1)
            nc.scalar.activation(tpow[:, :], tabs[:, :], ACT.Exp, scale=-1.0).then_inc(exp_loaded, 1)
            for n, (w, bank) in enumerate(((qk_w, psS), (vo_w, psP))):
                act.wait_ge(qkvo_mm, n + 1)
                nc.scalar.activation(w[:, :, :], bank[:, :], ACT.Copy).then_inc(qkvo_ready, 1)

            def copy(out, src, done, **kw):
                nc.scalar.activation(out, src, ACT.Copy, **kw).then_inc(done, 1)

            def normed_in(b):
                act.wait_ge(t1_mm, b + 1)
                if later(b):
                    act.wait_ge(s_mm, b)
                copy(xn_t[:, :, :], psT1[:, :], xnt_ready)

            def keys_in(b):
                act.wait_ge(g_mm, b + 1)
                copy(g_t[:, :, :], psG[:, :], gt_ready, scale=float(D) ** -0.5)

            def router_in(b):
                act.wait_ge(t2_mm, b + 1)
                if later(b):
                    act.wait_ge(r_mm, b)
                copy(xn2_t[:, :, :], psT2[:, :], xn2t_ready)

            def keep(b):
                act.wait_ge(xn2_ready, b * 2 + 2)
                copy(xn2_kept[:, bass.ds(b * 2, 2), :], xn2[:, :, :], kept)

            def probs_out(b):
                act.wait_ge(pt_mm, b + 1)
                if later(b):
                    act.wait_ge(pv_mm, b)
                copy(p_t[:, :], psP[:, 0:3 * P], pt_ready)

            def values(b):
                act.wait_ge(v_mm, b + 1)
                if later(b):
                    act.wait_ge(pv_mm, b)
                copy(v_b[:, :, :], psV[:, :], v_ready)

            def pick_ratio(j):
                act.wait_ge(gap_ready, j + 1)
                if later(j):
                    act.wait_ge(weights_ready, j)
                nc.scalar.activation(ratio[:, :], gap[:, :], ACT.Exp).then_inc(ratio_ready, 1)

            def fill_row(b, half, j):
                act.wait_ge(kept, b + 1)
                if later(j):
                    act.wait_ge(scattered[half], j * SENT)
                copy(row[half][:, :, 0:D], xn2_kept[:, bass.ds(b * 2, 2), :], row_filled)

            def softmax(b):
                act.wait_ge(nmax_ready, b + 1)
                if later(b):
                    act.wait_ge(pt_mm, b)
                    act.wait_ge(rinv_ready, b)
                nc.scalar.activation(p_b[:, 0:P], psS[:, 0:P], ACT.Exp, bias=nmax[:, 0:1],
                                     accum_out=rsum[:, 0:1]).then_inc(probs_ready, 1)
                nc.scalar.activation(p_b[:, P:3 * P], psS[:, P:3 * P], ACT.Exp, bias=nmax[:, 1:2],
                                     accum_out=rsum[:, 1:2]).then_inc(probs_ready, 1)

            def upper_spec(b):
                act.wait_ge(idft_mm, b)
                copy(spec_parts[MC:2 * MC, :], spec[:, bass.ds(b * SEQ, SEQ)], spec_upper_act)

            def act_slot(k, odd, j):
                if odd and on_pair(j):
                    pick_ratio(j)
                if on(k):
                    normed_in(k)
                if on(k - 1):
                    softmax(k - 1)
                if on(k - 2):
                    router_in(k - 2)
                if on(k - 1):
                    probs_out(k - 1)
                if on(k):
                    keys_in(k)
                if on(k - 2):
                    keep(k - 2)
                if on(k + 2):
                    upper_spec(k + 2)
                if on(k):
                    values(k)
                if on(k - 5):
                    fill_row(k - 5, 0 if odd else 1, j if odd else j - 1)

            run_attention(act, act_slot)

            def expert_of(g):
                return act.value_load(table[0:1, 0, bass.ds(g, 1)], min_val=0, max_val=E - 1)

            def fc_upper(g, par):
                e = expert_of(g)
                landed = act.value_load(table[0:1, 2, bass.ds(g, 1)], min_val=16, max_val=16 * E)
                if not isinstance(g, int) or g > 1:
                    act.wait_ge(up_mm, g * 4 - 4)
                act.wait_ge(ld_w, landed)
                for a in range(DH):
                    copy(fc_hi[par][:, a, :], w_ffn[:, bass.ds(e, 1), a * DFF:(a + 1) * DFF].rearrange("p a f -> p (a f)"),
                         fc_hi_ready)

            def proj_upper(g, a):
                e = expert_of(g)
                if later(g):
                    act.wait_ge(down_mm, g * 2 + a - 1)
                copy(pj_hi[:, 4 * a:4 * a + 4, :],
                     w_ffn[:, bass.ds(e, 1), (2 + a) * DFF:(3 + a) * DFF].rearrange("p a (c d) -> p (a c) d", d=D),
                     pj_hi_ready)

            def x_upper(g):
                act.wait_ge(xg_t_mm, g + 1)
                if later(g):
                    act.wait_ge(up_mm, g * 4)
                copy(x_hi[:, :, :], psS[:, :], x_hi_ready)

            def gelu(g, c):
                act.wait_ge(up_mm, g * 4 + c + 1)
                if c >= 2 or later(g):
                    act.wait_ge(h_ready, g * 4 + c - 1)
                nc.scalar.activation(h[:, c % 2, :, :], banks[c][:, :], ACT.Gelu).then_inc(gelu_done, 1)

            def outputs(g):
                act.wait_ge(down_mm, g * 2 + 2)
                if later(g):
                    act.wait_ge(y_added, g * 32)
                for s, bank in enumerate((psP, psO)):
                    nc.scalar.activation(y[:, s, :], bank[:, 0:D], ACT.Copy,
                                         scale=slot_w[:, bass.ds(g, 1), s]).then_inc(y_ready, 1)

            def act_group(g, par):
                if g_on(g + 1):
                    fc_upper(g + 1, 1 - par)
                gelu(g, 0)
                proj_upper(g, 1)
                gelu(g, 1)
                if g_on(g - 1):
                    outputs(g - 1)
                gelu(g, 2)
                gelu(g, 3)
                if g_on(g + 1):
                    x_upper(g + 1)
                if g_on(g + 2):
                    act.wait_ge(meta_read, g * 2 + 4)
                    act.sem_inc(act_passed, 1)
                    load_group(act, g + 2)
                if g_on(g + 1):
                    proj_upper(g + 1, 0)

            act.wait_ge(x2_stored, 16 * (B + 1))
            act.wait_ge(rows_ready, 1)
            for half in range(2):
                act.wait_ge(scattered[half], SENT * EARLY_PAIRS)
            act.wait_ge(idle_stored, 16)
            act.wait_ge(slots_complete, act.value_load(first_need[0:1, 0:1], min_val=1, max_val=2))
            act.sem_inc(act_passed, 1)
            load_group(act, 0)
            act.wait_ge(plan_ready, 2)
            fc_upper(0, 0)
            after_attention(act)
            x_upper(0)
            proj_upper(0, 0)
            run_groups(act, act_group)
            outputs(GROUPS - 1)

        @block.vector
        def _(dve):
            steps = [0]

            def link(ins):
                steps[0] += 1
                ins.then_inc(emb_step, 1)
                dve.wait_ge(emb_step, steps[0])

            v = nc.vector

            def alone(s, value):
                dve.wait_ge(s, value)
                dve.sem_inc(dve_passed, 1)

            dve.wait_ge(ld_emb, 16)
            a, turns, near = ang[:, 0, :], ang[:, 1, :], ang[:, 2, :]
            link(v.tensor_scalar(a, t_row[:, :], angles[:, 0:1], None, ALU.mult))
            link(v.tensor_scalar(turns, a, 1 / TWO_PI, MAGIC, ALU.mult, ALU.add))
            link(v.tensor_scalar(turns, turns, MAGIC, None, ALU.subtract))
            for turn in two_pi_parts():
                link(v.scalar_tensor_tensor(a, turns, -turn, a, ALU.mult, ALU.add))
            link(v.tensor_scalar(a, a, PI_LOW, -PI_LOW, ALU.min, ALU.max))
            link(v.scalar_tensor_tensor(near, a, -1.0, a, ALU.mult, ALU.min))
            link(v.tensor_scalar(near, near, np.pi / 2, angles[:, 2:3], ALU.add, ALU.mult))
            v.scalar_tensor_tensor(a, a, angles[:, 1:2], near, ALU.mult, ALU.add).then_inc(emb_ready, 1)
            dve.wait_ge(ld_conv, 16)
            flat = mixr_w[:, :, :, :].rearrange("p g o c -> p (g o) c")
            v.tensor_tensor(sq[:, :, :], flat, flat, ALU.mult).then_inc(wabs_step, 1)
            dve.wait_ge(wabs_step, 1)
            v.tensor_tensor(wsq[:, :], sq[:, :, 0], sq[:, :, 1], ALU.add).then_inc(wabs_step, 1)

            def time_weights():
                dve.wait_ge(temb_mm, 1)
                for c in range(2):
                    v.tensor_scalar(temb[:, c, :], psT1[:, c * HT:(c + 1) * HT], bias[:, c:c + 1], None,
                                    ALU.add).then_inc(temb_step, 1)
                dve.wait_ge(temb_step, 2)
                v.tensor_tensor(tsq[:, :, :], temb[:, :, :], temb[:, :, :], ALU.mult).then_inc(temb_step, 1)
                dve.wait_ge(temb_step, 3)
                v.tensor_tensor(tpow[:, :], tsq[:, 0, :], tsq[:, 1, :], ALU.add).then_inc(temb_step, 1)

            gn_steps = [0]

            def gn_link(ins):
                gn_steps[0] += 1
                ins.then_inc(gn_step, 1)
                dve.wait_ge(gn_step, gn_steps[0])

            def gn_statistics(c):
                dve.wait_ge(ld_xc[c], 16)
                for n in range(CT):
                    ins = v.bn_stats(gst[:, c, n, :], gn_tile(c, n))
                gn_link(ins)

            def gn_moments(c):
                for n in range(CT):
                    ins = v.bn_aggr(gmv[:, c, n, :], gst[:, c, n, :])
                gn_link(ins)
                mean, var = gmv[:, c, :, 0], gmv[:, c, :, 1]
                gn_link(v.tensor_tensor(gsq[:, c, :], mean, mean, ALU.mult))
                v.tensor_tensor(var, var, gsq[:, c, :], ALU.add).then_inc(gn_stats, 1)

            def gn_variance(c):
                dve.wait_ge(gn_mm, c + 1)
                gn_link(v.tensor_copy(ggm[:, c, :, :], psO[:, 0:2 * CT]))
                gn_link(v.tensor_tensor(gsq[:, c, :], ggm[:, c, :, 0], ggm[:, c, :, 0], ALU.mult))
                gn_link(v.tensor_tensor(gvar[:, c, :], ggm[:, c, :, 1], gsq[:, c, :], ALU.subtract))
                v.tensor_scalar(gvar[:, c, :], gvar[:, c, :], GN_EPS, None, ALU.add).then_inc(gn_var, 1)

            def gn_scale(c):
                dve.wait_ge(gn_sd, c + 1)
                gn_link(v.reciprocal(grs[:, c, :], gsd[:, c, :]))
                v.scalar_tensor_tensor(gnb[:, c, :], ggm[:, c, :, 0], -1.0, grs[:, c, :], ALU.mult, ALU.mult).then_inc(gn_rs, 1)

            gn_statistics(0)
            gn_moments(0)
            dve.wait_ge(wabs_ready, 1)
            v.tensor_reduce(wabs_sum[:, :], wabs[:, :].rearrange("p (g o) -> p o g", g=NG), AX_X, ALU.add).then_inc(wabs_summed, 1)
            time_weights()
            for c in range(1, CHUNKS):
                gn_statistics(c)
                gn_variance(c - 1)
                gn_moments(c)
                gn_scale(c - 1)
            gn_variance(CHUNKS - 1)
            dve.wait_ge(norm_mm, 1)
            v.tensor_scalar(inv[:, :], psI[:, 0:NG * HT], 1e-12, 1.0, ALU.add, ALU.max).then_inc(inv_step, 1)
            dve.wait_ge(inv_step, 1)
            v.reciprocal(inv[:, :], inv[:, :]).then_inc(inv_ready, 1)
            gn_scale(CHUNKS - 1)
            dve.wait_ge(gn_rs, CHUNKS)
            for n in range(CT // 2, CT):
                tile = gn_tile(CHUNKS - 1, n)
                v.tensor_scalar(tile, tile, ggm[:, CHUNKS - 1, n, 0:1], grs[:, CHUNKS - 1, n:n + 1], ALU.subtract,
                                ALU.mult).then_inc(gn_done_dve, 1)
            dve.wait_ge(ld_attn, 16)
            v.tensor_copy(causal_16[:, :], causal).then_inc(mask_ready, 1)
            v.tensor_copy(ident_16[:, :], ident_in).then_inc(mask_ready, 1)
            for g in range(NG):
                dve.wait_ge(dft_mm, g + 1)
                for z, c in ((zr, 0), (zi, 1)):
                    v.tensor_tensor(z[:, g, :, :], banks[g][:, 0:B * HT],
                                    temb[:, c:c + 1, :].broadcast_to([P, B, HT]), ALU.mult).then_inc(z_ready, 1)
            dve.wait_ge(inv_ready, 1)
            for o in range(WI):
                og, j = o // 4, o % 4
                if j == 0:
                    dve.wait_ge(mix_mm, og + 1)
                rows = slice(32 * j, 32 * j + 32)
                v.tensor_tensor(spec[:, :].rearrange("p (b t o) -> p b t o", b=B, o=WI)[:, :, :, o],
                                banks[4 + og][rows, 0:B * HT],
                                inv[rows, og * HT:(og + 1) * HT].unsqueeze(1).broadcast_to([32, B, HT]),
                                ALU.mult).then_inc(spec_ready, 1)

            def tiles_of(b):
                return x[:, bass.ds(b * 2, 2), :]

            def conv_out(b):
                dve.wait_ge(idft_mm, b + 1)
                v.tensor_tensor(tiles_of(b), psI[:, :], tiles_of(b), ALU.add).then_inc(x1_ready, 1)

            def sums_inverse(b):
                dve.wait_ge(probs_ready, b * 2 + 2)
                v.reciprocal(rinv[:, :], rsum[:, :]).then_inc(rinv_ready, 1)

            def attn_out(b):
                dve.wait_ge(pv_mm, b + 1)
                dve.wait_ge(rinv_ready, b + 1)
                rows = tiles_of(b)
                for s in range(2):
                    v.scalar_tensor_tensor(rows[:, s, :], psO[:, s * D:(s + 1) * D], rinv[:, s:s + 1], rows[:, s, :],
                                           ALU.mult, ALU.add).then_inc(x2_ready, 1)

            def variances(b, norm):
                t = NORM_TILES[norm]
                alone(stats_ready[norm], b + 1)
                for n in range(t.start, t.stop):
                    ins = v.bn_aggr(mv[:, n, :], st[:, n, :])
                ins.then_inc(mv_ready[norm], 1)
                dve.wait_ge(mv_ready[norm], b + 1)
                v.tensor_scalar(rs[:, t], mv[:, t, 1], LN_EPS, None, ALU.add).then_inc(var_ready[norm], 1)

            def normed(b, first, out, ready):
                rows = tiles_of(b)
                for s in range(2):
                    n = first + s
                    v.tensor_scalar(out[:, s, :], rows[:, s, :], mv[:, n, 0:1], rs[:, n:n + 1],
                                    ALU.subtract, ALU.mult).then_inc(ready, 1)

            def highest(b):
                dve.wait_ge(s_mm, b + 1)
                if later(b):
                    dve.wait_ge(probs_ready, b * 2)
                v.tensor_reduce(nmax[:, 0:1], psS[:, 0:P], AX_X, ALU.max, negate=True)
                v.tensor_reduce(nmax[:, 1:2], psS[:, P:3 * P], AX_X, ALU.max, negate=True).then_inc(nmax_ready, 1)

            def wide(a):
                return a.unsqueeze(2).broadcast_to([P, PT, E])

            def logits_in(b, half, where_too):
                dve.wait_ge(r_mm, b + 1)
                if where_too is not None:
                    dve.wait_ge(where_mm, where_too + 1)
                v.tensor_copy(logits[:, 2 * half:2 * half + 2, :], psT2[:, 0:2 * E]).then_inc(logits_ready, 1)

            def pick(j):
                STEPS = 11
                count = [0]

                def then(ins):
                    count[0] += 1
                    ins.then_inc(top_step, 1)
                    dve.wait_ge(top_step, j * STEPS + count[0])

                left = logits[:, :, :]
                dve.wait_ge(logits_ready, j * 2 + 2)
                for n in range(PICKS):
                    then(v.tensor_reduce(best[:, n, :], left, AX_X, ALU.max))
                    then(v.tensor_tensor(cand[:, :, :], left, wide(best[:, n, :]), ALU.is_equal))
                    then(v.tensor_tensor(cand[:, :, :], cand[:, :, :], experts[:, 0], ALU.mult))
                    then(v.tensor_reduce(key[:, :], cand[:, :, :], AX_X, ALU.max))
                    then(v.tensor_tensor(hot[:, n], cand[:, :, :], wide(key[:, :]), ALU.is_equal))
                    if n == 0:
                        then(v.scalar_tensor_tensor(rest[:, :, :], hot[:, 0], -3e38, left, ALU.mult, ALU.add))
                        left = rest[:, :, :]
                if later(j):
                    dve.wait_ge(ratio_ready, j)
                v.tensor_tensor(gap[:, :], best[:, 1, :], best[:, 0, :], ALU.subtract).then_inc(gap_ready, 1)
                assert count[0] == STEPS

            def count_picks(j):
                if later(j):
                    dve.wait_ge(where_mm, j)
                    v.tensor_tensor(before[:, 0], before[:, PT - 1], picked[:, PT - 1], ALU.add).then_inc(before_ready, 1)
                else:
                    v.memset(before[:, 0], 0.0).then_inc(before_ready, 1)
                dve.wait_ge(before_ready, j * (PT + 1) + 1)
                v.tensor_tensor(picked[:, :, :], hot[:, 0], hot[:, 1], ALU.add).then_inc(before_ready, 1)
                for t in range(1, PT):
                    dve.wait_ge(before_ready, j * (PT + 1) + t + 1)
                    v.tensor_tensor(before[:, t], before[:, t - 1], picked[:, t - 1], ALU.add).then_inc(before_ready, 1)

            def weigh(j):
                STEPS = 5
                count = [0]

                def then(ins):
                    count[0] += 1
                    ins.then_inc(pick_step, 1)
                    dve.wait_ge(pick_step, j * STEPS + count[0])

                dve.wait_ge(ratio_ready, j + 1)
                then(v.tensor_scalar(pick_w[:, 0, :], ratio[:, :], 1.0, None, ALU.add))
                then(v.reciprocal(pick_w[:, 0, :], pick_w[:, 0, :]))
                then(v.tensor_tensor(pick_w[:, 1, :], ratio[:, :], pick_w[:, 0, :], ALU.mult))
                v.tensor_tensor(part[:, 0], hot[:, 0], wide(pick_w[:, 0, :]), ALU.mult).then_inc(pick_step, 1)
                count[0] += 1
                then(v.tensor_tensor(part[:, 1], hot[:, 1], wide(pick_w[:, 1, :]), ALU.mult))
                assert count[0] == STEPS
                if later(j):
                    dve.wait_ge(row_ready, j * 4)
                v.tensor_tensor(weights[:, :, :], part[:, 0], part[:, 1], ALU.add).then_inc(weights_ready, 1)
                dve.wait_ge(weights_ready, j + 1)

            def find_slots(j):
                dve.wait_ge(where_mm, j + 1)
                v.tensor_tensor(where[:, :, :], counts_bank(j)[:, WHERE:WHERE + PT * E], experts[:, 1], ALU.add).then_inc(where_read, 1)
                dve.wait_ge(where_read, j + 1)
                for n in range(PICKS):
                    v.tensor_tensor(part[:, n], hot[:, n], where[:, :, :], ALU.mult).then_inc(slot_step, 1)
                dve.wait_ge(slot_step, j * 3 + 2)
                v.tensor_reduce(slot_f[:, :, :], part[:, :, :, :], AX_X, ALU.add).then_inc(slot_step, 1)
                dve.wait_ge(slot_step, j * 3 + 3)
                if later(j) and slots_of(j) is slot:
                    for half in range(2):
                        dve.wait_ge(scattered[half], j * SENT)
                    dve.sem_inc(dve_passed, 1)
                v.tensor_copy(slots_of(j)[:, :, :], slot_f[:, :, :]).then_inc(slot_ready, 1)

            def need_of_first():
                v.tensor_scalar(need[:, :], where[:, 0, 0:1], float(GS), -1.0,
                                ALU.is_ge, ALU.mult).then_inc(need_step, 1)
                dve.wait_ge(need_step, 1)
                v.tensor_scalar(need[:, :], need[:, :], 2.0, None, ALU.add).then_inc(need_step, 1)
                dve.wait_ge(need_step, 2)
                v.tensor_copy(first_need[:, :], need[:, :]).then_inc(need_step, 1)

            def dve_slot(k, odd, j):
                if isinstance(k, int) and (k + 1) * 2 == NT // 4:
                    dve.wait_ge(ld_x[1], 16)
                if on(k + 1):
                    conv_out(k + 1)
                if on(k - 1):
                    sums_inverse(k - 1)
                if on(k + 1):
                    alone(x1_ready, k + 2)
                    rows = tiles_of(k + 1)
                    for s in range(2):
                        ins = v.bn_stats(st[:, s, :], rows[:, s, :])
                    ins.then_inc(stats_ready[0], 1)
                    variances(k + 1, 0)
                if on_pair(j):
                    if odd:
                        weigh(j)
                    else:
                        pick(j)
                if on(k + 1):
                    dve.wait_ge(rs_ready[0], k + 2)
                    if later(k + 1):
                        dve.wait_ge(t1_mm, k + 1)
                    normed(k + 1, 0, xn, xn_ready)
                if on(k - 1):
                    attn_out(k - 1)
                    rows = tiles_of(k - 1)
                    for s in range(2):
                        alone(x2_ready, k * 2 + s - 1)
                        ins = v.bn_stats(st[:, 2 + s, :], rows[:, s, :])
                    ins.then_inc(stats_ready[1], 1)
                    variances(k - 1, 1)
                if ending(j) and odd and on_pair(j):
                    find_slots(j)
                    if j == EARLY_PAIRS:
                        need_of_first()
                if on(k - 2):
                    logits_in(k - 2, odd, j if odd and on_pair(j) and not ending(j) else None)
                if on_pair(j):
                    if not odd:
                        count_picks(j)
                    elif not ending(j):
                        find_slots(j)
                if on(k - 1):
                    dve.wait_ge(rs_ready[1], k)
                    if later(k - 1):
                        dve.wait_ge(t2_mm, k - 1)
                        dve.wait_ge(kept, k - 1)
                    normed(k - 1, 2, xn2, xn2_ready)
                if on(k):
                    highest(k)

            dve.wait_ge(spec_ready, WI)
            v.tensor_copy(spec_parts[0:MC, :], spec[:, 0:SEQ]).then_inc(spec_upper, 1)
            v.tensor_copy(spec_parts[MC:2 * MC, :], spec[:, 0:SEQ]).then_inc(spec_upper_act, 1)
            dve.wait_ge(spec_upper, 1)
            v.tensor_tensor(spec_parts[2 * MC:, :], spec[:, 0:SEQ], spec_parts[0:MC, :].bitcast(F32),
                            ALU.subtract).then_inc(spec_lower, 1)
            dve.wait_ge(ld_x[0], 16)
            run_attention(dve, dve_slot)

            plan_steps = [0]

            def step(ins):
                plan_steps[0] += 1
                ins.then_inc(plan_step, 1)
                dve.wait_ge(plan_step, plan_steps[0])

            n_slots, n_groups, ends, ones = counts[:, 0], counts[:, 1], counts[:, 2], counts[:, 3]
            step(v.tensor_tensor(before[:, 0], before[:, PT - 1], picked[:, PT - 1], ALU.add))
            v.memset(ones, 1.0).then_inc(ones_ready, 1)
            dve.wait_ge(ones_ready, 1)
            dve.wait_ge(counts_mm, 1)
            step(v.tensor_copy(n_slots, psS[:, 0:E]))
            step(v.tensor_tensor(tail_f[:, :], n_slots, experts[:, 1, 0, :], ALU.add))
            v.tensor_copy(tail[:, :], tail_f[:, :]).then_inc(plan_ready, 1)
            step(v.tensor_scalar(n_groups, n_slots, 1.0 / GS, 127.5 / GS, ALU.mult, ALU.add))
            step(v.tensor_scalar(n_groups, n_groups, MAGIC, None, ALU.add))
            step(v.tensor_scalar(n_groups, n_groups, MAGIC, None, ALU.subtract))
            step(v.tensor_tensor_scan(ends, ones, n_groups, 0.0, ALU.mult, ALU.add))
            dve.wait_ge(ld_numbers, 16)
            all_ends = ends.unsqueeze(1).broadcast_to([P, GROUPS, E])
            step(v.tensor_tensor(past[:, :, :], numbers[:, :, :], all_ends, ALU.is_ge))
            step(v.tensor_tensor(past_end[:, :, :], past[:, :, :], all_ends, ALU.mult))
            step(v.tensor_reduce(plan[:, 0, :], past[:, :, :], AX_X, ALU.add))
            step(v.tensor_reduce(plan[:, 1, :], past_end[:, :, :], AX_X, ALU.max))
            step(v.tensor_tensor(plan[:, 1, :], numbers[:, :, 0], plan[:, 1, :], ALU.subtract))
            step(v.tensor_scalar(plan[:, 2, :], plan[:, 0, :], float(E), float(GS), ALU.is_lt, ALU.mult))
            step(v.tensor_tensor(plan[:, 1, :], plan[:, 1, :], plan[:, 2, :], ALU.mult))
            step(v.scalar_tensor_tensor(plan[:, 1, :], plan[:, 0, :], float(REGION), plan[:, 1, :], ALU.mult, ALU.add))
            v.tensor_copy(table[:, 1, :], plan[:, 1, :]).then_inc(rows_ready, 1)
            step(v.tensor_scalar(plan[:, 3, :], plan[:, 0, :], float(E - 1), None, ALU.min))
            step(v.tensor_copy(table[:, 3, :], plan[:, 3, :]))
            step(v.tensor_scalar(plan[:, 2, :], plan[:, 3, :], float(E - LATE), float(-E), ALU.is_ge, ALU.mult))
            step(v.scalar_tensor_tensor(plan[:, 2, :], plan[:, 3, :], float(LATE), plan[:, 2, :], ALU.add, ALU.add))
            step(v.tensor_copy(table[:, 0, :], plan[:, 2, :]))
            step(v.tensor_scalar(plan[:, 3, :], plan[:, 3, :], 16.0, 16.0, ALU.mult, ALU.add))
            v.tensor_copy(table[:, 2, :], plan[:, 3, :]).then_inc(plan_ready, 1)
            for n in range(LATE - 1):
                first = ends[:, E - LATE + n - 1:E - LATE + n]
                step(v.tensor_scalar(behind_f[:, n:n + 1], first, 1.0, float(LATE_BEHIND[n]), ALU.max, ALU.min))
            step(v.tensor_scalar(behind_f[:, :], behind_f[:, :], 16.0, None, ALU.mult))
            v.tensor_copy(late_need[:, :], behind_f[:, :]).then_inc(late_ready, 1)

            def expert_of(g):
                return dve.value_load(table[0:1, 0, bass.ds(g, 1)], min_val=0, max_val=E - 1)

            def lower(out, whole, upper, done):
                v.tensor_tensor(out, whole, upper.bitcast(F32), ALU.subtract).then_inc(done, 1)

            def fc_lower(g, par, e):
                for a in range(DH):
                    dve.wait_ge(fc_hi_ready, g * 2 + a + 1)
                    lower(fc_lo[par][:, a, :], w_ffn[:, bass.ds(e, 1), a * DFF:(a + 1) * DFF].rearrange("p a f -> p (a f)"),
                          fc_hi[par][:, a, :], fc_lo_ready)

            def x_lower(g):
                dve.wait_ge(x_hi_ready, g + 1)
                lower(x_lo[:, :, :], psS[:, :].rearrange("p (h n) -> p h n", h=DH), x_hi[:, :, :], x_lo_ready)

            def hidden(g, c):
                dve.wait_ge(gelu_done, g * 4 + c + 1)
                v.tensor_copy(h_hi[:, 2 * c:2 * c + 2, :], h[:, c % 2]).then_inc(h_hi_ready, 1)
                dve.wait_ge(h_hi_ready, g * 4 + c + 1)
                lower(h_lo[:, 2 * c:2 * c + 2, :], h[:, c % 2], h_hi[:, 2 * c:2 * c + 2, :], h_ready)

            def slot_meta(g):
                at = dve.value_load(table[0:1, 3, bass.ds(g, 1)], min_val=0, max_val=E - 1) + ROW_W
                alone(xg_loaded, g * 16 + 16)
                v.tensor_copy(slot_w[:, bass.ds(g, 1), :].rearrange("p a s -> p s a"), xg[:, :, bass.ds(at, 1)]).then_inc(meta_read, 1)
                v.tensor_copy(slot_id[:, bass.ds(g, 1), :].rearrange("p a s -> p s a"),
                              xg[:, :, ROW_ID:ROW_ID + 1].bitcast(I32)).then_inc(meta_read, 1)

            def dve_group(g, par):
                if g_on(g + 1):
                    fc_lower(g + 1, 1 - par, expert_of(g + 1))
                hidden(g, 0)
                hidden(g, 1)
                if g_on(g + 1):
                    slot_meta(g + 1)
                hidden(g, 2)
                hidden(g, 3)
                if g_on(g + 1):
                    x_lower(g + 1)

            after_attention(dve)
            dve.sem_inc(dve_passed, 1)
            first_expert = expert_of(0)
            slot_meta(0)
            fc_lower(0, 0, first_expert)
            x_lower(0)
            run_groups(dve, dve_group)

        @block.tensor
        def _(pe):
            mm = nc.tensor.matmul
            pe.wait_ge(ld_emb, 16)
            pe.wait_ge(sin_ready, 1)
            mm(psT1[:, 0:HT], temb_rw[:, :], emb[:, :], start=True, stop=True)
            mm(psT1[:, HT:2 * HT], temb_iw[:, :], emb[:, :], start=True, stop=True).then_inc(temb_mm, 1)
            pe.wait_ge(ld_conv, 16)

            def group_means(c):
                pe.wait_ge(gn_stats, c + 1)
                if c:
                    pe.wait_ge(gn_var, c)
                mm(psO[:, 0:2 * CT], group[:, :], gmv[:, c, :, :], start=True, stop=True).then_inc(gn_mm, 1)

            def fold(w, m, bank):
                for a in range(DH):
                    for e in range(DH):
                        ins = mm(bank[:, a * D:(a + 1) * D], w[:, e, a * P:(a + 1) * P], m[:, e, :],
                                 start=(e == 0), stop=(e == DH - 1))
                ins.then_inc(qkvo_mm, 1)

            def spectra(half):
                cols = slice(half * SEQ // 2, (half + 1) * SEQ // 2)
                for g in range(NG):
                    for j in range(4):
                        for hh in range(DH):
                            ins = mm(banks[g][32 * j:32 * j + 32, cols], dft[:, hh, :],
                                     xc[:, hh, :].rearrange("p (n i) -> p i n", i=WI)[:, 4 * g + j, cols],
                                     start=(hh == 0), stop=(hh == DH - 1))
                    if half:
                        ins.then_inc(dft_mm, 1)

            for c in range(CHUNKS - 1):
                group_means(c)
            pe.wait_ge(mix_built, 2 * NG + 1)
            pe.wait_ge(temb_ready, 1)
            for og in range(NG):
                ins = mm(psI[:, og * HT:(og + 1) * HT],
                         mix_abs[:, og * 4:(og + 1) * 4].rearrange("p o x c -> p (o x c)"), tabs[:, :],
                         start=True, stop=True)
            ins.then_inc(norm_mm, 1)
            group_means(CHUNKS - 1)
            pe.wait_ge(temb_step, 2)
            pe.wait_ge(gn_done, 2 * CT)
            spectra(0)
            pe.wait_ge(gn_done, 3 * CT + CT // 2)
            pe.wait_ge(gn_done_dve, CT // 2)
            spectra(1)
            pe.wait_ge(gn_var, CHUNKS)
            pe.wait_ge(inv_step, 1)
            for og in range(NG):
                for g in range(NG):
                    for n, (w, z) in enumerate(((mix_r, zr), (mix_i, zi))):
                        if og == 0:
                            pe.wait_ge(z_ready, 2 * g + n + 1)
                        ins = mm(banks[4 + og][:, 0:B * HT],
                                 w[:, g, og * 4:(og + 1) * 4].rearrange("p o x c -> p (o x c)"),
                                 z[:, g].rearrange("p b t -> p (b t)"), start=(g == 0 and n == 0),
                                 stop=(g == NG - 1 and n == 1))
                ins.then_inc(mix_mm, 1)

            pe.wait_ge(ld_attn, 16)
            pe.wait_ge(ld_ident, 16)
            pe.wait_ge(idft_ready, 2)

            def idft_of(b):
                pe.wait_ge(spec_upper_act, b + 1)
                pe.wait_ge(spec_lower, b + 1)
                if later(b):
                    pe.wait_ge(x1_ready, b)
                for s in range(2):
                    ins = mm(psI[:, s * D:(s + 1) * D], spec_parts[:, s * P:(s + 1) * P], idft_parts[:, :], start=True, stop=True)
                ins.then_inc(idft_mm, 1)

            def transposes(b, rows, bank, ready, done, bank_read, pairs_read=None):
                pe.wait_ge(ready, b * 2 + 2)
                if later(b):
                    pe.wait_ge(bank_read, b)
                if pairs_read is not None:
                    pe.wait_ge(where_read, pairs_read)
                for hh in range(DH):
                    for s in range(2):
                        ins = nc.tensor.transpose(bank[:, hh * SEQ + s * P:hh * SEQ + (s + 1) * P],
                                                  rows[:, s, hh * P:(hh + 1) * P], ident[:, :])
                ins.then_inc(done, 1)

            def query_keys(b):
                pe.wait_ge(xnt_ready, b + 1)
                if later(b):
                    pe.wait_ge(gt_ready, b)
                for a in range(DH):
                    for hh in range(DH):
                        ins = mm(psG[:, a * SEQ:(a + 1) * SEQ], qk_w[:, hh, a * P:(a + 1) * P], xn_t[:, hh, :],
                                 start=(hh == 0), stop=(hh == DH - 1))
                ins.then_inc(g_mm, 1)

            def values(b):
                pe.wait_ge(xnt_ready, b + 1)
                if later(b):
                    pe.wait_ge(v_ready, b)
                for s in range(2):
                    for hh in range(DH):
                        ins = mm(psV[:, s * D:(s + 1) * D], xn_t[:, hh, s * P:(s + 1) * P], vo_w[:, hh, :],
                                 start=(hh == 0), stop=(hh == DH - 1))
                ins.then_inc(v_mm, 1)

            def route(b):
                pe.wait_ge(xn2t_ready, b + 1)
                for s in range(2):
                    for hh in range(DH):
                        ins = mm(psT2[:, s * E:(s + 1) * E], xn2_t[:, hh, s * P:(s + 1) * P],
                                 router[:, hh, :], start=(hh == 0), stop=(hh == DH - 1))
                ins.then_inc(r_mm, 1)

            def count_before(j):
                pe.wait_ge(before_ready, (j + 1) * (PT + 1))
                if ending(j):
                    pe.wait_ge(gt_ready, B)
                    pe.wait_ge(where_read, j)
                bank = counts_bank(j)[:, WHERE:WHERE + PT * E]
                mm(bank, counting[:, 0, :], picked[:, :, :], start=True, stop=False)
                mm(bank, counting[:, 1, :], before[:, :, :], start=False, stop=True).then_inc(where_mm, 1)

            def scores(b):
                pe.wait_ge(gt_ready, b + 1)
                if later(b):
                    pe.wait_ge(probs_ready, b * 2)
                for s in range(2):
                    block = psS[:, s * P:(2 * s + 1) * P]
                    q = [g_t[:, hh, s * P:(s + 1) * P] for hh in range(DH)]
                    keys = [xn_t[:, hh, 0:(s + 1) * P] for hh in range(DH)]
                    mm(block, q[0], keys[0], start=True, stop=False)
                    mm(block[:, s * P:(s + 1) * P], ident_16[:, :], causal_16[:, :], start=False, stop=False)
                    ins = mm(block, q[1], keys[1], start=False, stop=True)
                ins.then_inc(s_mm, 1)

            def probs_t(b):
                pe.wait_ge(probs_ready, b * 2 + 2)
                if later(b):
                    pe.wait_ge(pt_ready, b)
                for n in range(3):
                    ins = nc.tensor.transpose(psP[:, n * P:(n + 1) * P], p_b[:, n * P:(n + 1) * P], ident[:, :])
                ins.then_inc(pt_mm, 1)

            def attend(b):
                pe.wait_ge(pt_ready, b + 1)
                pe.wait_ge(v_ready, b + 1)
                if later(b):
                    pe.wait_ge(x2_ready, b * 2)
                mm(psO[:, 0:D], p_t[:, 0:P], v_b[:, 0, :], start=True, stop=True)
                mm(psO[:, D:2 * D], p_t[:, P:2 * P], v_b[:, 0, :], start=True, stop=False)
                mm(psO[:, D:2 * D], p_t[:, 2 * P:3 * P], v_b[:, 1, :], start=False, stop=True).then_inc(pv_mm, 1)

            def pe_slot(k, odd, j):
                if isinstance(k, int) and k == 0:
                    fold(wv, wo_t, psP)
                    pe.wait_ge(qkvo_ready, 2)
                if on(k):
                    transposes(k, xn, psT1, xn_ready, t1_mm, xnt_ready)
                if on(k + 1):
                    idft_of(k + 1)
                if odd and on_pair(j) and ending(j):
                    count_before(j)
                if on(k - 2):
                    transposes(k - 2, xn2, psT2, xn2_ready, t2_mm, logits_ready, None if odd or not on_pair(j - 1) else j)
                if on(k):
                    query_keys(k)
                if on(k - 1):
                    probs_t(k - 1)
                if on(k - 2):
                    route(k - 2)
                if odd and on_pair(j) and not ending(j):
                    count_before(j)
                if on(k - 1):
                    attend(k - 1)
                if on(k):
                    values(k)
                    scores(k)

            pe.wait_ge(ld_qkvo, 16)
            pe.wait_ge(spec_ready, 4)
            fold(wq, wk, psS)
            pe.wait_ge(mask_ready, 2)
            run_attention(pe, pe_slot)
            pe.wait_ge(plan_step, 1)
            pe.wait_ge(where_read, PAIRS)
            mm(psS[:, 0:E], counting[:, 1, :], before[:, 0], start=True, stop=True).then_inc(counts_mm, 1)

            def three(w_hi, w_lo, m_hi, m_lo):
                return (w_hi, m_hi), (w_hi, m_lo), (w_lo, m_hi)

            def x_transposes(g):
                pe.wait_ge(xg_loaded, g * 16 + 16)
                if later(g):
                    pe.wait_ge(x_lo_ready, g)
                for hh in range(DH):
                    for s in range(2):
                        ins = nc.tensor.transpose(psS[:, hh * GS + s * P:hh * GS + (s + 1) * P],
                                                  xg[:, s, hh * P:(hh + 1) * P], ident[:, :])
                ins.then_inc(xg_t_mm, 1)

            def up(g, par):
                pe.wait_ge(x_lo_ready, g + 1)
                pe.wait_ge(fc_lo_ready, g * 2 + 2)
                for f in range(FC):
                    c = f // 2
                    if f % 2 == 0 and later(g):
                        pe.wait_ge(gelu_done, g * 4 + c - 3)
                    n = 0
                    for w, m in three(fc_hi[par], fc_lo[par], x_hi, x_lo):
                        for hh in range(DH):
                            ins = mm(banks[c][:, (f % 2) * GS:(f % 2 + 1) * GS], w[:, hh, f * P:(f + 1) * P], m[:, hh, :],
                                     start=(n == 0), stop=(n == 5))
                            n += 1
                    if f % 2:
                        ins.then_inc(up_mm, 1)

            def down(g):
                if later(g):
                    pe.wait_ge(y_ready, g * 2)
                for f in range(FC):
                    if f % 4 == 0:
                        pe.wait_ge(pj_lo_ready, g * 2 + f // 4 + 1)
                    if f % 2 == 0:
                        pe.wait_ge(h_ready, g * 4 + f // 2 + 1)
                    for s, bank in enumerate((psP, psO)):
                        for n, (w, m) in enumerate(three(h_hi, h_lo, pj_hi, pj_lo)):
                            ins = mm(bank[:, 0:D], w[:, f, s * P:(s + 1) * P], m[:, f, :],
                                     start=(f == 0 and n == 0), stop=(f == FC - 1 and n == 2))
                    if f % 4 == 3:
                        ins.then_inc(down_mm, 1)

            def pe_group(g, par):
                up(g, par)
                if g_on(g + 1):
                    x_transposes(g + 1)
                down(g)

            x_transposes(0)
            run_groups(pe, pe_group)


def laid_out(i):
    f = {n: np.asarray(a) for n, a in i.items()}
    flat = f["x"].reshape(TOK, D)
    w = f["L0_conv_weights1"]
    swapped = w[..., ::-1]
    mixr = np.stack([w, swapped], axis=3)
    mixi = np.stack([swapped, w], axis=3)

    def rows(a):
        return np.ascontiguousarray(a.transpose(0, 2, 3, 1, 4).reshape(NG, P, WI, 2).transpose(1, 0, 2, 3))

    ke = f["L0_conv_ke_weights"]
    temb_w = []
    for c in range(2):
        full = np.zeros((HEADS, MIDCH // HEADS, HEADS, MODES, 2), ke.dtype)
        for hd in range(HEADS):
            full[hd, :, hd] = ke[hd, :, c::2, None]
        temb_w.append(full.reshape(MIDCH, P))
    kb = f["L0_conv_ke_bias"].reshape(MODES, 2)
    bias = np.broadcast_to(kb[None, :, None, :], (4, MODES, 2, 2)).reshape(P, 2)
    w_fc = f["L1_ffn_w_fc"].reshape(E, DH, P, DFF).transpose(0, 2, 1, 3).reshape(E, P, DH * DFF)
    w_proj = f["L1_ffn_w_proj"].reshape(E, FC, P, D).transpose(0, 2, 1, 3).reshape(E, P, FC * D)
    w_ffn = np.concatenate([w_fc, w_proj], axis=2)
    c = constants()
    time_in = np.concatenate([*temb_w, c.pop("angles"), np.broadcast_to(f["L0_conv_t"][None], (MIDCH, HT))], axis=1)
    conv_in = np.concatenate([rows(mixr).reshape(P, -1), rows(mixi).reshape(P, -1), c.pop("masks").reshape(P, -1),
                              c.pop("dft").reshape(DH, P, MC).transpose(1, 0, 2).reshape(P, -1), c.pop("group"), bias], axis=1)
    w_in = np.stack([f["L1_attn_W_q"], f["L1_attn_W_k"], f["L1_attn_W_v"], f["L1_attn_W_o"].T])
    w_in = w_in.reshape(4, DH, P, D).transpose(2, 0, 1, 3)
    router = f["L1_ffn_router_w"].reshape(DH, P, E).transpose(1, 0, 2)
    attn_in = np.concatenate([c["ident"], c.pop("causal"), c.pop("counting").reshape(P, -1), c.pop("experts").reshape(P, -1),
                              router.reshape(P, -1)], axis=1)
    return {"x_tok": flat, "x_ch": flat.T, "time_in": time_in, "conv_in": conv_in, "w_in": w_in, "attn_in": attn_in,
            "w_ffn": w_ffn, **c}


def kernel(**inputs):
    import concourse.bacc as bacc
    from concourse.bass_utils import run_bass_kernel_spmd

    nc = bacc.Bacc("TRN2", target_bir_lowering=False, num_devices=1)
    arrays, args = {}, []
    for name, a in laid_out(inputs).items():
        a = np.ascontiguousarray(a)
        arrays["in_" + name] = a
        args.append(nc.dram_tensor("in_" + name, a.shape, mybir.dt.from_np(a.dtype), kind="ExternalInput").ap())
    args.append(nc.dram_tensor("out", (TOK + GS, D), F32, kind="ExternalOutput").ap())
    args.append(nc.dram_tensor("slots", (IDLE_ROW + GS, ROW), F32, kind="Internal").ap())
    hybrid_block(nc, *args)
    r = run_bass_kernel_spmd(nc, [arrays], core_ids=[0])
    return r.results[0]["out"][:TOK].reshape(B, HT, WI, D)
```
